# Optimizing a Trainium2 kernel written in Bass

```python
import numpy as np
import jax
import jax.numpy as jnp

def _softmax(x, axis=-1):
    return jax.nn.softmax(x, axis=axis)

def _gelu(x):
    return jax.nn.gelu(x, approximate=True)

def _silu(x):
    return jax.nn.silu(x)

def _sigmoid(x):
    return jax.nn.sigmoid(x)

def _layernorm(x, axis=-1, eps=1e-05):
    m = jnp.mean(x, axis=axis, keepdims=True)
    v = jnp.var(x, axis=axis, keepdims=True)
    return (x - m) / jnp.sqrt(v + eps)

def _scatter_add(tgt, idx, src, axis=0):
    return tgt.at[idx].add(src)

def _segment_sum(src, seg, n):
    return jax.ops.segment_sum(src, seg, n)
kernel_name = 'mk_xattn_seq_d1_seqx_r4_bcb896'

def setup_inputs(seed: int=0):
    np.random.seed(seed)
    _w = jnp.asarray

    def _rec_inputs():
        import jax
        import jax.numpy as jnp
        _rk = jax.random.key(seed)
        x = -0.0009896 + 1 * jax.random.normal(jax.random.fold_in(_rk, 1), (8, 256, 256), jnp.float32)
        _lenS = 256 - jax.random.randint(jax.random.fold_in(_rk, 7), (8,), 0, max(1, 256 // 4) + 1, jnp.int32)
        _lenS2 = 256 - jax.random.randint(jax.random.fold_in(_rk, 8), (8,), 0, max(1, 256 // 4) + 1, jnp.int32)
        _ctx_768P = jax.random.normal(jax.random.fold_in(_rk, 11), (8, 16, 192), jnp.float32)
        _ctx_768c = jax.random.dirichlet(jax.random.fold_in(_rk, 511), 0.3 * jnp.ones((16,), jnp.float32), (8, 256))
        _ctx_768t = jnp.einsum('bsk,bkd->bsd', _ctx_768c, _ctx_768P)
        _ctx_768t = _ctx_768t * jax.lax.rsqrt(jnp.mean(jnp.square(_ctx_768t)) + 1e-12) * 0.953939
        ctx_768 = 0.00095986 + 0.999812 * (_ctx_768t + 0.3 * jax.random.normal(jax.random.fold_in(_rk, 611), (8, 256, 192), jnp.float32))
        _validS = jnp.arange(256)[None, :] < _lenS[:, None]
        _validS2 = jnp.arange(256)[None, :] < _lenS2[:, None]
        _causal = jnp.tril(jnp.ones((256, 256), dtype=bool))
        mask_BxS2_if1 = jnp.where(jnp.ones((8, 256), dtype=bool), 1, 0).astype(jnp.int32)
        return (x, ctx_768, mask_BxS2_if1)
    x, ctx_768, mask_BxS2_if1 = _rec_inputs()

    def _L0_xattn_setup():
        import jax, jax.numpy as jnp
        import numpy as np
        import math
        H = 8
        D = 256
        D_I = 256
        D_L = 192
        EPS = 1e-05
        key = jax.random.key(seed)
        ks = jax.random.split(key, 8)
        B, NQ, NK = (8, 196, 128)
        img_embed = jax.random.normal(ks[0], (B, NQ, D_I), dtype=jnp.float32)
        sent_embed = jax.random.normal(ks[1], (B, NK, D_L), dtype=jnp.float32)
        atten_mask = jnp.ones((B, NK), dtype=jnp.int32)
        Wq = jax.random.normal(ks[2], (D_I, H * D), dtype=jnp.float32) * (1.0 / math.sqrt(D_I))
        Wk = jax.random.normal(ks[3], (D_L, H * D), dtype=jnp.float32) * (1.0 / math.sqrt(D_L))
        Wv = jax.random.normal(ks[4], (D_L, H * D), dtype=jnp.float32) * (1.0 / math.sqrt(D_L))
        Wo = jax.random.normal(ks[5], (H * D, D_I), dtype=jnp.float32) * (1.0 / math.sqrt(H * D))
        gamma = jnp.ones((D_I,), dtype=jnp.float32)
        beta = jnp.zeros((D_I,), dtype=jnp.float32)
        return {'img_embed': img_embed, 'sent_embed': sent_embed, 'atten_mask': atten_mask, 'Wq': Wq, 'Wk': Wk, 'Wv': Wv, 'Wo': Wo, 'gamma': gamma, 'beta': beta}
    _L0_xattn_all = _L0_xattn_setup()
    _L0_xattn_in = {k: v for k, v in _L0_xattn_all.items() if k in ('Wq', 'Wk', 'Wv', 'Wo', 'gamma', 'beta')}
    del _L0_xattn_all
    return {'x': x, 'ctx_768': ctx_768, 'mask_BxS2_if1': mask_BxS2_if1, 'L0_xattn_Wq': _L0_xattn_in['Wq'], 'L0_xattn_Wk': _L0_xattn_in['Wk'], 'L0_xattn_Wv': _L0_xattn_in['Wv'], 'L0_xattn_Wo': _L0_xattn_in['Wo'], 'L0_xattn_gamma': _L0_xattn_in['gamma'], 'L0_xattn_beta': _L0_xattn_in['beta']}

def reference(x, ctx_768, mask_BxS2_if1, L0_xattn_Wq, L0_xattn_Wk, L0_xattn_Wv, L0_xattn_Wo, L0_xattn_gamma, L0_xattn_beta):
    import jax
    import jax.numpy as jnp

    def _L0_xattn_ref(img_embed, sent_embed, atten_mask, Wq, Wk, Wv, Wo, gamma, beta):
        import jax, jax.numpy as jnp
        import numpy as np
        import math
        H = 8
        D = 256
        D_I = 256
        D_L = 192
        EPS = 1e-05
        B = img_embed.shape[0]
        Q = (img_embed @ Wq).reshape(B, -1, H, D).transpose(0, 2, 1, 3)
        K = (sent_embed @ Wk).reshape(B, -1, H, D).transpose(0, 2, 1, 3)
        V = (sent_embed @ Wv).reshape(B, -1, H, D).transpose(0, 2, 1, 3)
        score = jnp.einsum('bhqd,bhkd->bhqk', Q, K) / math.sqrt(D)
        mask = (atten_mask != 0)[:, None, None, :]
        score = jnp.where(mask, score, -jnp.inf)
        attn = jax.nn.softmax(score, axis=-1)
        ctx = jnp.einsum('bhqk,bhkd->bqhd', attn, V).reshape(B, -1, H * D)
        out = ctx @ Wo + img_embed
        mu = jnp.mean(out, axis=-1, keepdims=True)
        var = jnp.var(out, axis=-1, keepdims=True)
        return (out - mu) * jax.lax.rsqrt(var + EPS) * gamma + beta
    x = _L0_xattn_ref(x, ctx_768, mask_BxS2_if1, L0_xattn_Wq, L0_xattn_Wk, L0_xattn_Wv, L0_xattn_Wo, L0_xattn_gamma, L0_xattn_beta)
    return x

_drawn_inputs = setup_inputs


def setup_inputs(seed=0):
    import zlib

    import numpy as np

    out = dict(_drawn_inputs(seed))
    spreads = {'L0_xattn_gamma': (1.0, 0.2), 'L0_xattn_beta': (0.0, 0.1)}
    factors = {}
    for name, (base, spread) in spreads.items():
        noise = np.random.default_rng([zlib.crc32(name.encode()), seed]).standard_normal(out[name].shape)
        drawn = base * np.exp(spread * noise) if base else spread * noise
        out[name] = jnp.asarray(drawn.astype(out[name].dtype))
    for name, factor in factors.items():
        out[name] = (out[name] * factor).astype(out[name].dtype)
    return out
```

```python
from contextlib import ExitStack

import numpy as np

import concourse.bass as bass
from concourse import mybir

F32 = mybir.dt.float32
F32R = mybir.dt.float32r
I32 = mybir.dt.int32
ALU = mybir.AluOpType
ACT = mybir.ActivationFunctionType

P = 128
B = 8
S = 256
KV = 256
H = 8
D = 256
DI = 256
DL = 192
EPS = 1e-5
SCALE = 1.0 / D ** 0.5

UP = DL - P
PAIRS = H // 2
STEPS = B * PAIRS
QT = S // P
KT = KV // P
IT = DI // P
DT = D // P
PW = 2 * P + 2 * UP
MASKED = -3.0e38



def attention_kernel(nc, xT, x, ctxT, ctx, mask, wqT, wkT, wvT, wo, gamma, beta, out):
    es = ExitStack()
    with es:
        def sb(name, shape, dt=F32):
            return es.enter_context(nc.sbuf_tensor(name, shape, dt))

        def bank(name, shape):
            return es.enter_context(nc.psum_tensor(name, shape, F32))

        def sem(name):
            return es.enter_context(nc.semaphore(name))

        wq_raw = sb("wq_raw", [P, H * DT, DI])
        wk_raw = sb("wk_raw", [P, H * DT, DL])
        wv_raw = sb("wv_raw", [P, H * DT, DL])
        wo_raw = sb("wo_raw", [P, H * DT, DI])
        A_hi = sb("A_hi", [P, IT, PAIRS * PW], F32R)
        A_lo = sb("A_lo", [P, IT, PAIRS * PW], F32R)
        CL_hi = sb("CL_hi", [P, H, DI], F32R)
        CL_lo = sb("CL_lo", [P, H, DI], F32R)
        CU_hi = sb("CU_hi", [P, PAIRS, DI], F32R)
        CU_lo = sb("CU_lo", [P, PAIRS, DI], F32R)
        gamma_sb = sb("gamma_sb", [P, DI])
        beta_sb = sb("beta_sb", [P, DI])
        ident = sb("ident", [P, P])
        eps_col = sb("eps_col", [P, QT])
        power_col = sb("power_col", [P, QT])

        xT_raw = sb("xT_raw", [P, IT, S])
        xT_hi = sb("xT_hi", [P, IT, S], F32R)
        xT_lo = sb("xT_lo", [P, IT, S], F32R)
        ctxT_raw = sb("ctxT_raw", [P, 2, KV])
        ctxT_hi = sb("ctxT_hi", [P, 2, KV], F32R)
        ctxT_lo = sb("ctxT_lo", [P, 2, KV], F32R)
        ctx_raw = sb("ctx_raw", [P, KT, DL])
        ctxL_hi = sb("ctxL_hi", [P, KT, P], F32R)
        ctxL_lo = sb("ctxL_lo", [P, KT, P], F32R)
        ctxU_hi = sb("ctxU_hi", [P, KT, 3 * UP], F32R)
        ctxU_lo = sb("ctxU_lo", [P, KT, 3 * UP], F32R)
        mask_raw = sb("mask_raw", [P, KV], I32)
        mask_low = sb("mask_low", [P, KV])
        mask_bias = sb("mask_bias", [P, KV])
        x_res = sb("x_res", [P, QT, DI])

        gL_hi = sb("gL_hi", [P, 2, S], F32R)
        gL_lo = sb("gL_lo", [P, 2, S], F32R)
        gU = sb("gU", [P, 2, S], F32R)
        neg_scores = sb("neg_scores", [P, 2 * QT, KV])
        neg_max = sb("neg_max", [P, 2 * QT])
        probs = sb("probs", [P, 2 * QT, KV])
        row_sum = sb("row_sum", [P, 2 * QT])
        inv_sum = sb("inv_sum", [P, 2 * QT])
        pT_hi = sb("pT_hi", [P, KT, 2, S], F32R)
        pT_lo = sb("pT_lo", [P, KT, 2, S], F32R)
        tL_hi = sb("tL_hi", [P, 2, S], F32R)
        tL_lo = sb("tL_lo", [P, 2, S], F32R)
        tU_hi = sb("tU_hi", [P, S], F32R)
        tU_lo = sb("tU_lo", [P, S], F32R)

        y = sb("y", [P, QT, DI])
        y_scaled = sb("y_scaled", [P, QT, DI])
        y_out = sb("y_out", [P, QT, DI])
        stats = sb("stats", [P, QT, 6])
        mean_var = sb("mean_var", [P, QT, 2])
        var_eps = sb("var_eps", [P, QT])
        rstd = sb("rstd", [P, QT])

        score_bank = [bank("score_bank0", [P, QT, KV]), bank("score_bank1", [P, QT, KV])]
        pT_bank = [bank("pT_bank0", [P, KT, S]), bank("pT_bank1", [P, KT, S])]
        tL_bank = bank("tL_bank", [P, 2, S])
        tU_bank = bank("tU_bank", [P, 2, S])
        gL_bank = bank("gL_bank", [P, 2, S])
        out_bank = bank("out_bank", [P, QT, DI])
        gU_bank = score_bank[1]
        fold_banks = [pT_bank[0], pT_bank[1], tL_bank, tU_bank]

        q_weights_in = [sem(f"q_weights_in{j}") for j in range(PAIRS)]
        o_weights_in = [sem(f"o_weights_in{j}") for j in range(PAIRS)]
        affine_in = sem("affine_in")
        xT_in = sem("xT_in")
        ctxT_in = sem("ctxT_in")
        ctx_in = sem("ctx_in")
        mask_in = sem("mask_in")
        x_res_in = sem("x_res_in")
        out_stored = sem("out_stored")
        constants = sem("constants")
        pads_zeroed = sem("pads_zeroed")
        A_product = sem("A_product")
        A_hi_done = sem("A_hi_done")
        A_split = sem("A_split")
        C_product = sem("C_product")
        C_hi_done = sem("C_hi_done")
        C_split = sem("C_split")
        xT_hi_done = sem("xT_hi_done")
        xT_split = sem("xT_split")
        ctxT_hi_done = sem("ctxT_hi_done")
        ctxT_split = sem("ctxT_split")
        ctx_hi_done = sem("ctx_hi_done")
        ctx_split = sem("ctx_split")
        mask_lowered = sem("mask_lowered")
        mask_ready = sem("mask_ready")
        g_product = sem("g_product")
        g_hi_done = sem("g_hi_done")
        g_split = sem("g_split")
        scores_done = sem("scores_done")
        max_done = sem("max_done")
        exp_done = sem("exp_done")
        inv_done = sem("inv_done")
        probs_done = sem("probs_done")
        pT_done = sem("pT_done")
        pT_hi_done = sem("pT_hi_done")
        pT_split = sem("pT_split")
        t_product = sem("t_product")
        t_hi_done = sem("t_hi_done")
        t_split = sem("t_split")
        out_product = sem("out_product")
        out_bank_read = sem("out_bank_read")
        stats_done = sem("stats_done")
        mean_done = sem("mean_done")
        var_eps_done = sem("var_eps_done")
        rstd_done = sem("rstd_done")
        y_scaled_done = sem("y_scaled_done")
        y_out_done = sem("y_out_done")

        waits_passed = sem("waits_passed")

        block = es.enter_context(nc.Block())

        def batch_of(src, b):
            if isinstance(b, int):
                return src[b]
            return src[bass.ds(b, 1)].rearrange("o p a c -> p (o a) c")

        @block.sync
        def _(sp):
            def load_xT(b):
                sp.dma_start(xT_raw[:], batch_of(xT, b)).then_inc(xT_in, 16)

            def load_ctxT(b):
                sp.dma_start(ctxT_raw[:], batch_of(ctxT, b)).then_inc(ctxT_in, 16)

            def load_ctx(b):
                sp.dma_start(ctx_raw[:], batch_of(ctx, b)).then_inc(ctx_in, 16)

            def load_x_res(b):
                sp.dma_start(x_res[:], batch_of(x, b)).then_inc(x_res_in, 16)

            def load_mask(b):
                src = mask[b:b + 1] if isinstance(b, int) else mask[bass.ds(b, 1)]
                sp.dma_start(mask_raw[:], src.broadcast_to((P, KV))).then_inc(mask_in, 16)

            def store_out(b):
                sp.wait_ge(y_out_done, QT * b + QT)
                sp.dma_start(batch_of(out, b), y_out[:]).then_inc(out_stored, 16)

            sp.sem_inc(out_stored, 16)
            per = 2 * DT
            for j in range(PAIRS):
                tiles = slice(j * per, (j + 1) * per)
                sp.dma_start(wk_raw[:, tiles], wkT[:, tiles]).then_inc(q_weights_in[j], 16)
                sp.dma_start(wq_raw[:, tiles], wqT[:, tiles]).then_inc(q_weights_in[j], 16)
                if j == 0:
                    load_xT(0)
            load_ctxT(0)
            load_mask(0)
            load_ctx(0)
            for j in range(PAIRS):
                tiles = slice(j * per, (j + 1) * per)
                sp.dma_start(wv_raw[:, tiles], wvT[:, tiles]).then_inc(o_weights_in[j], 16)
                sp.dma_start(wo_raw[:, tiles], wo[:, tiles]).then_inc(o_weights_in[j], 16)
            load_x_res(0)
            sp.dma_start(gamma_sb[:], gamma.broadcast_to((P, DI))).then_inc(affine_in, 16)
            sp.dma_start(beta_sb[:], beta.broadcast_to((P, DI))).then_inc(affine_in, 16)

            with sp.Fori(0, B - 1) as b:
                sp.wait_ge(xT_split, b + 1)
                load_xT(b + 1)
                sp.wait_ge(ctxT_split, b + 1)
                load_ctxT(b + 1)
                sp.wait_ge(mask_lowered, b + 1)
                load_mask(b + 1)
                sp.wait_ge(ctx_split, 2 * b + 2)
                load_ctx(b + 1)
                sp.wait_ge(out_bank_read, b + 2)
                load_x_res(b + 1)
                store_out(b)
            store_out(B - 1)
            sp.wait_ge(out_stored, 16 * B + 16)

        @block.tensor
        def _(pe):
            def split_products(into, pairs, first=True, last=True, shared=False):
                for n, (stationary, moving) in enumerate(pairs):
                    ins = nc.tensor.matmul(into, stationary, moving, start=first and n == 0,
                                           stop=last and n == len(pairs) - 1, skip_group_check=shared)
                return ins

            def fold_A(h):
                if h % 2 == 0:
                    pe.wait_ge(q_weights_in[h // 2], 32)
                if h >= len(fold_banks):
                    pe.wait_ge(A_split, 2 * (h - len(fold_banks)) + 2)
                dst = fold_banks[h % len(fold_banks)][:].rearrange("p a c -> p (a c)")
                for i in range(IT):
                    for d in range(DT):
                        ins = nc.tensor.matmul(dst[:, i * DL:(i + 1) * DL],
                                               wq_raw[:, h * DT + d, i * P:(i + 1) * P],
                                               wk_raw[:, h * DT + d, :], start=d == 0, stop=d == DT - 1)
                ins.then_inc(A_product, 1)

            def fold_C(j):
                pe.wait_ge(o_weights_in[j], 32)
                if j == 0:
                    pe.wait_ge(A_split, 2 * H)
                if j >= 2:
                    pe.wait_ge(C_split, 2 * (j - 2) + 2)
                lower, upper = fold_banks[2 * (j % 2)], fold_banks[2 * (j % 2) + 1]
                for hh in range(2):
                    h = 2 * j + hh
                    for d in range(DT):
                        ins = nc.tensor.matmul(lower[:, hh, :], wv_raw[:, h * DT + d, 0:P],
                                               wo_raw[:, h * DT + d, :], start=d == 0, stop=d == DT - 1)
                ins.then_inc(C_product, 1)
                for hh in range(2):
                    h = 2 * j + hh
                    for d in range(DT):
                        ins = nc.tensor.matmul(upper[hh * UP:(hh + 1) * UP, 0, :],
                                               wv_raw[:, h * DT + d, P:DL],
                                               wo_raw[:, h * DT + d, :], start=d == 0, stop=d == DT - 1)
                ins.then_inc(C_product, 1)

            def query_products(t, j, b):
                if j == 0:
                    pe.wait_ge(xT_split, b + 1)
                col = j * PW

                def tile(into, at):
                    pairs = []
                    for i in range(IT):
                        hi, lo = A_hi[:, i, at:at + P], A_lo[:, i, at:at + P]
                        pairs += [(hi, xT_hi[:, i, :]), (hi, xT_lo[:, i, :]), (lo, xT_hi[:, i, :])]
                    return split_products(into, pairs)

                tile(gL_bank[:, 0, :], col)
                tile(gL_bank[:, 1, :], col + P).then_inc(g_product, 1)
                if not (isinstance(t, int) and t == 0):
                    pe.wait_ge(max_done, 4 * t)
                tile(gU_bank[:, 0, :], col + 2 * P).then_inc(g_product, 1)

            def scores(t, j, b):
                if j == 0:
                    pe.wait_ge(ctxT_split, b + 1)
                for hh in range(2):
                    pe.wait_ge(g_split, 3 * t + 2 + hh)
                    for q in range(QT):
                        rows = slice(q * P, (q + 1) * P)
                        hi, lo, up = gL_hi[:, hh, rows], gL_lo[:, hh, rows], gU[:, hh, rows]
                        ins = split_products(score_bank[hh][:, q, :],
                                             [(hi, ctxT_hi[:, 0, :]), (hi, ctxT_lo[:, 0, :]), (lo, ctxT_hi[:, 0, :]),
                                              (up, ctxT_hi[:, 1, :]), (up, ctxT_lo[:, 1, :])])
                    ins.then_inc(scores_done, 1)

            def transposes(t):
                for hh in range(2):
                    pe.wait_ge(probs_done, 2 * t + 1 + hh)
                    for k in range(KT):
                        for q in range(QT):
                            ins = nc.tensor.transpose(pT_bank[hh][:, k, q * P:(q + 1) * P],
                                                      probs[:, hh * QT + q, k * P:(k + 1) * P], ident[:])
                    ins.then_inc(pT_done, 1)

            def context_products(t, j, b):
                if j == 0:
                    pe.wait_ge(ctx_split, 2 * b + 2)
                pe.wait_ge(pT_split, 2 * t + 2)
                pairs = []
                for k in range(KT):
                    hi, lo = ctxL_hi[:, k, :], ctxL_lo[:, k, :]
                    pairs += [(hi, pT_hi[:, k]), (hi, pT_lo[:, k]), (lo, pT_hi[:, k])]
                split_products(tL_bank[:], pairs).then_inc(t_product, 1)
                pairs = []
                for hh in range(2):
                    cols = slice(UP, 3 * UP) if hh == 0 else slice(0, 2 * UP)
                    for k in range(KT):
                        hi, lo = ctxU_hi[:, k, cols], ctxU_lo[:, k, cols]
                        pairs += [(hi, pT_hi[:, k, hh]), (hi, pT_lo[:, k, hh]), (lo, pT_hi[:, k, hh])]
                split_products(tU_bank[:, 0, :], pairs).then_inc(t_product, 1)

            def output_products(t, j, b):
                if j == 0:
                    pe.wait_ge(out_bank_read, b + 1)
                pe.wait_ge(t_split, 2 * t + 2)
                for q in range(QT):
                    rows = slice(q * P, (q + 1) * P)
                    pairs = []
                    for hh in range(2):
                        hi, lo, h = tL_hi[:, hh, rows], tL_lo[:, hh, rows], 2 * j + hh
                        pairs += [(hi, CL_hi[:, h]), (hi, CL_lo[:, h]), (lo, CL_hi[:, h])]
                    hi, lo = tU_hi[:, rows], tU_lo[:, rows]
                    pairs += [(hi, CU_hi[:, j]), (hi, CU_lo[:, j]), (lo, CU_hi[:, j])]
                    ins = split_products(out_bank[:, q, :], pairs, first=j == 0 and q == 0,
                                         last=j == PAIRS - 1, shared=True)
                ins.then_inc(out_product, 1)

            def step(t, j, b, before=True, after=True):
                jb, bb = (j - 1) % PAIRS, b - 1 if j == 0 else b
                ja, ba = (j + 1) % PAIRS, b + 1 if j == PAIRS - 1 else b
                if before:
                    transposes(t - 1)
                scores(t, j, b)
                if before:
                    context_products(t - 1, jb, bb)
                if after:
                    query_products(t + 1, ja, ba)
                if before:
                    output_products(t - 1, jb, bb)

            for h in range(H):
                fold_A(h)
            pe.wait_ge(A_split, 2 * H)
            query_products(0, 0, 0)
            step(0, 0, 0, before=False)
            for j in range(PAIRS):
                fold_C(j)
            pe.wait_ge(constants, 3)
            pe.wait_ge(C_split, 2 * PAIRS)
            with pe.Fori(0, B - 1) as b:
                for j in range(1, PAIRS):
                    step(PAIRS * b + j, j, b)
                step(PAIRS * b + PAIRS, 0, b + 1)
            for j in range(1, PAIRS):
                step(STEPS - PAIRS + j, j, B - 1, after=j < PAIRS - 1)
            transposes(STEPS - 1)
            context_products(STEPS - 1, PAIRS - 1, B - 1)
            output_products(STEPS - 1, PAIRS - 1, B - 1)

        @block.scalar
        def _(act):
            def hi_part(dst, src):
                return nc.scalar.activation(dst, src, ACT.Copy)

            def A_hi_part(h):
                act.wait_ge(A_product, h + 1)
                src = fold_banks[h % len(fold_banks)][:].rearrange("p a c -> p (a c)")[:, 0:IT * DL] \
                    .rearrange("p (i f) -> p i f", i=IT)
                low = (h // 2) * PW + (h % 2) * P
                up = (h // 2) * PW + 2 * P + (h % 2) * UP
                hi_part(A_hi[:, :, low:low + P], src[:, :, 0:P]).then_inc(A_hi_done, 1)
                hi_part(A_hi[:, :, up:up + UP], src[:, :, P:DL]).then_inc(A_hi_done, 1)

            def C_hi_part(j):
                lower, upper = fold_banks[2 * (j % 2)], fold_banks[2 * (j % 2) + 1]
                act.wait_ge(C_product, 2 * j + 1)
                hi_part(CL_hi[:, 2 * j:2 * j + 2, :], lower[:]).then_inc(C_hi_done, 1)
                act.wait_ge(C_product, 2 * j + 2)
                hi_part(CU_hi[:, j, :], upper[:, 0, :]).then_inc(C_hi_done, 1)

            def xT_hi_part(b):
                act.wait_ge(xT_in, 16 * b + 16)
                hi_part(xT_hi[:], xT_raw[:]).then_inc(xT_hi_done, 1)

            def ctxT_hi_part(b):
                act.wait_ge(ctxT_in, 16 * b + 16)
                hi_part(ctxT_hi[:], ctxT_raw[:]).then_inc(ctxT_hi_done, 1)

            def ctx_hi_part(b):
                act.wait_ge(ctx_in, 16 * b + 16)
                hi_part(ctxL_hi[:], ctx_raw[:, :, 0:P]).then_inc(ctx_hi_done, 1)
                hi_part(ctxU_hi[:, :, UP:2 * UP], ctx_raw[:, :, P:DL]).then_inc(ctx_hi_done, 1)

            def g_hi_part(t):
                act.wait_ge(g_product, 2 * t + 1)
                hi_part(gL_hi[:], gL_bank[:]).then_inc(g_hi_done, 1)
                act.wait_ge(g_product, 2 * t + 2)
                hi_part(gU[0:UP, 0, :], gU_bank[0:UP, 0, :]).then_inc(g_hi_done, 1)
                hi_part(gU[UP:P, 1, :], gU_bank[UP:P, 0, :]).then_inc(g_hi_done, 1)

            def exponentials(t):
                for n in range(2 * QT):
                    act.wait_ge(max_done, 4 * t + 1 + n)
                    nc.scalar.activation(probs[:, n, :], neg_scores[:, n, :], ACT.Exp,
                                         bias=neg_max[:, n:n + 1], scale=-1.0,
                                         accum_out=row_sum[:, n:n + 1]).then_inc(exp_done, 1)

            def pT_hi_part(t):
                for hh in range(2):
                    act.wait_ge(pT_done, 2 * t + 1 + hh)
                    hi_part(pT_hi[:, :, hh, :], pT_bank[hh][:]).then_inc(pT_hi_done, 1)

            def t_hi_part(t):
                act.wait_ge(t_product, 2 * t + 1)
                hi_part(tL_hi[:], tL_bank[:]).then_inc(t_hi_done, 1)
                act.wait_ge(t_product, 2 * t + 2)
                hi_part(tU_hi[:], tU_bank[:, 0, :]).then_inc(t_hi_done, 1)

            def step(t, j, b, before=True, after=True):
                if before:
                    pT_hi_part(t - 1)
                if j == PAIRS - 1 and after:
                    xT_hi_part(b + 1)
                exponentials(t)
                if before:
                    t_hi_part(t - 1)
                if j == PAIRS - 1 and after:
                    ctxT_hi_part(b + 1)
                if j == 0 and before:
                    ctx_hi_part(b)
                if after:
                    g_hi_part(t + 1)

            for h in range(H):
                A_hi_part(h)
            xT_hi_part(0)
            g_hi_part(0)
            ctxT_hi_part(0)
            step(0, 0, 0, before=False)
            ctx_hi_part(0)
            for j in range(PAIRS):
                C_hi_part(j)
            with act.Fori(0, B - 1) as b:
                for j in range(1, PAIRS):
                    step(PAIRS * b + j, j, b)
                step(PAIRS * b + PAIRS, 0, b + 1)
            for j in range(1, PAIRS):
                step(STEPS - PAIRS + j, j, B - 1, after=j < PAIRS - 1)
            pT_hi_part(STEPS - 1)
            t_hi_part(STEPS - 1)

        @block.vector
        def _(dve):
            def waited():
                dve.sem_inc(waits_passed, 1)

            def lo_part(dst, whole, hi):
                return nc.vector.tensor_tensor(dst, whole, hi.bitcast(F32), ALU.subtract)

            def A_lo_part(h):
                src = fold_banks[h % len(fold_banks)][:].rearrange("p a c -> p (a c)")[:, 0:IT * DL] \
                    .rearrange("p (i f) -> p i f", i=IT)
                low = (h // 2) * PW + (h % 2) * P
                up = (h // 2) * PW + 2 * P + (h % 2) * UP
                dve.wait_ge(A_hi_done, 2 * h + 2)
                lo_part(A_lo[:, :, low:low + P], src[:, :, 0:P], A_hi[:, :, low:low + P]).then_inc(A_split, 1)
                lo_part(A_lo[:, :, up:up + UP], src[:, :, P:DL], A_hi[:, :, up:up + UP]).then_inc(A_split, 1)

            def C_lo_part(j):
                lower, upper = fold_banks[2 * (j % 2)], fold_banks[2 * (j % 2) + 1]
                dve.wait_ge(C_hi_done, 2 * j + 1)
                lo_part(CL_lo[:, 2 * j:2 * j + 2, :], lower[:], CL_hi[:, 2 * j:2 * j + 2, :]).then_inc(C_split, 1)
                dve.wait_ge(C_hi_done, 2 * j + 2)
                lo_part(CU_lo[:, j, :], upper[:, 0, :], CU_hi[:, j, :]).then_inc(C_split, 1)

            def xT_lo_part(b):
                dve.wait_ge(xT_hi_done, b + 1)
                lo_part(xT_lo[:], xT_raw[:], xT_hi[:]).then_inc(xT_split, 1)

            def ctxT_lo_part(b):
                dve.wait_ge(ctxT_hi_done, b + 1)
                lo_part(ctxT_lo[:], ctxT_raw[:], ctxT_hi[:]).then_inc(ctxT_split, 1)

            def ctx_lo_part(b):
                dve.wait_ge(ctx_hi_done, 2 * b + 2)
                lo_part(ctxL_lo[:], ctx_raw[:, :, 0:P], ctxL_hi[:]).then_inc(ctx_split, 1)
                lo_part(ctxU_lo[:, :, UP:2 * UP], ctx_raw[:, :, P:DL],
                        ctxU_hi[:, :, UP:2 * UP]).then_inc(ctx_split, 1)

            def mask_part(b):
                dve.wait_ge(mask_in, 16 * b + 16)
                nc.vector.tensor_scalar(mask_low[:], mask_raw[:], 0, MASKED, ALU.is_equal,
                                        ALU.mult).then_inc(mask_lowered, 1)
                dve.wait_ge(mask_lowered, b + 1)
                nc.vector.tensor_scalar(mask_bias[:], mask_low[:], 4.0, None, ALU.mult).then_inc(mask_ready, 1)

            def g_lo_part(t):
                dve.wait_ge(g_hi_done, 3 * t + 1)
                lo_part(gL_lo[:], gL_bank[:], gL_hi[:]).then_inc(g_split, 1)
                dve.wait_ge(g_hi_done, 3 * t + 3)
                lo_part(gU[UP:P, 0, :], gU_bank[0:UP, 0, :], gU[0:UP, 0, :]).then_inc(g_split, 1)
                lo_part(gU[0:UP, 1, :], gU_bank[UP:P, 0, :], gU[UP:P, 1, :]).then_inc(g_split, 1)

            def maxima(t, b):
                for hh in range(2):
                    dve.wait_ge(mask_ready, b + 1)
                    dve.wait_ge(scores_done, 2 * t + 1 + hh)
                    waited()
                    for q in range(QT):
                        n = hh * QT + q
                        nc.vector.tensor_tensor_reduce(
                            out=neg_scores[:, n, :], in0=score_bank[hh][:, q, :], in1=mask_bias[:],
                            scale=-SCALE, scalar=3.0e38, op0=ALU.add, op1=ALU.min,
                            accum_out=neg_max[:, n:n + 1]).then_inc(max_done, 1)

            def inverse_sum(t, hh):
                dve.wait_ge(exp_done, 4 * t + QT * (hh + 1))
                nc.vector.reciprocal(inv_sum[:, QT * hh:QT * hh + QT],
                                     row_sum[:, QT * hh:QT * hh + QT]).then_inc(inv_done, 1)

            def pT_lo_part(t):
                for hh in range(2):
                    dve.wait_ge(pT_hi_done, 2 * t + 1 + hh)
                    lo_part(pT_lo[:, :, hh, :], pT_bank[hh][:], pT_hi[:, :, hh, :]).then_inc(pT_split, 1)

            def t_lo_part_lower(t):
                dve.wait_ge(t_hi_done, 2 * t + 1)
                lo_part(tL_lo[:], tL_bank[:], tL_hi[:]).then_inc(t_split, 1)

            def t_lo_part_upper(t):
                dve.wait_ge(t_hi_done, 2 * t + 2)
                lo_part(tU_lo[:], tU_bank[:, 0, :], tU_hi[:]).then_inc(t_split, 1)

            def residual_and_statistics(b):
                dve.wait_ge(x_res_in, 16 * b + 16)
                dve.wait_ge(out_product, PAIRS * b + PAIRS)
                nc.vector.tensor_tensor(y[:], out_bank[:], x_res[:], ALU.add).then_inc(out_bank_read, 1)
                dve.wait_ge(out_bank_read, b + 2)
                for q in range(QT):
                    nc.vector.bn_stats(stats[:, q, :], y[:, q, :]).then_inc(stats_done, 1)
                for q in range(QT):
                    dve.wait_ge(stats_done, QT * b + q + 1)
                    waited()
                    nc.vector.bn_aggr(mean_var[:, q, :], stats[:, q, :]).then_inc(mean_done, 1)

            def normalise(b):
                for q in range(QT):
                    if q == 0:
                        dve.wait_ge(mean_done, QT * b + QT)
                        dve.wait_ge(rstd_done, b + 1)
                    nc.vector.scalar_tensor_tensor(
                        y_scaled[:, q, :], y[:, q, :], mean_var[:, q, 0:1], gamma_sb[:],
                        ALU.subtract, ALU.mult).then_inc(y_scaled_done, 1)
                dve.wait_ge(out_stored, 16 * b + 16)
                for q in range(QT):
                    dve.wait_ge(y_scaled_done, QT * b + q + 1)
                    nc.vector.scalar_tensor_tensor(
                        y_out[:, q, :], y_scaled[:, q, :], rstd[:, q:q + 1], beta_sb[:],
                        ALU.mult, ALU.add).then_inc(y_out_done, 1)

            def step(t, j, b, before=True, after=True, ends=None):
                if before:
                    pT_lo_part(t - 1)
                if j == PAIRS - 1 and after:
                    xT_lo_part(b + 1)
                maxima(t, b)
                inverse_sum(t, 0)
                if before:
                    t_lo_part_lower(t - 1)
                inverse_sum(t, 1)
                if before:
                    t_lo_part_upper(t - 1)
                if j == PAIRS - 1 and after:
                    ctxT_lo_part(b + 1)
                    mask_part(b + 1)
                if j == 0 and before:
                    ctx_lo_part(b)
                if after:
                    g_lo_part(t + 1)
                if ends is not None:
                    normalise(ends)
                if j == 0 and before:
                    residual_and_statistics(b - 1)

            dve.sem_inc(out_bank_read, 1)
            for part in (ctxU_hi, ctxU_lo):
                nc.vector.memset(part[:].bitcast(F32), 0.0).then_inc(pads_zeroed, 1)
            for h in range(H):
                A_lo_part(h)
            xT_lo_part(0)
            g_lo_part(0)
            ctxT_lo_part(0)
            mask_part(0)
            step(0, 0, 0, before=False)
            ctx_lo_part(0)
            for j in range(PAIRS):
                C_lo_part(j)
            dve.wait_ge(affine_in, 32)
            step(1, 1, 0)
            with dve.Fori(0, B - 1) as b:
                step(PAIRS * b + 2, 2, b)
                step(PAIRS * b + 3, 3, b)
                step(PAIRS * b + 4, 0, b + 1)
                step(PAIRS * b + 5, 1, b + 1, ends=b)
            step(STEPS - 2, 2, B - 1)
            step(STEPS - 1, 3, B - 1, after=False)
            pT_lo_part(STEPS - 1)
            t_lo_part_lower(STEPS - 1)
            t_lo_part_upper(STEPS - 1)
            residual_and_statistics(B - 1)
            normalise(B - 1)

        @block.gpsimd
        def _(pool):
            nc.gpsimd.memset(ident[:], 0.0).then_inc(constants, 1)
            nc.gpsimd.memset(eps_col[:], EPS)
            nc.gpsimd.memset(power_col[:], -0.5).then_inc(constants, 1)
            pool.wait_ge(constants, 2)
            nc.gpsimd.affine_select(out=ident[:], in_=ident[:], compare_op=ALU.not_equal, fill=1.0, base=0,
                                    pattern=[[-1, P]], channel_multiplier=1).then_inc(constants, 1)

            def normalise_probs(t):
                for hh in range(2):
                    rows = slice(QT * hh, QT * hh + QT)
                    inv = inv_sum[:, rows].rearrange("p (n o) -> p n o", o=1).broadcast_to((P, QT, KV))
                    pool.wait_ge(inv_done, 2 * t + 1 + hh)
                    nc.gpsimd.tensor_tensor(probs[:, rows, :], probs[:, rows, :], inv, ALU.mult) \
                        .then_inc(probs_done, 1)

            def deviation(b):
                pool.wait_ge(mean_done, QT * b + QT)
                nc.gpsimd.tensor_tensor(var_eps[:], mean_var[:, :, 1], eps_col[:], ALU.add).then_inc(var_eps_done, 1)
                pool.wait_ge(var_eps_done, b + 1)
                nc.gpsimd.tensor_tensor(rstd[:], var_eps[:], power_col[:], ALU.pow).then_inc(rstd_done, 1)

            for j in range(PAIRS + 1):
                normalise_probs(j)
            with pool.Fori(1, B - 1) as b:
                deviation(b - 1)
                for j in range(1, PAIRS + 1):
                    normalise_probs(PAIRS * b + j)
            deviation(B - 2)
            for j in range(1, PAIRS):
                normalise_probs(STEPS - PAIRS + j)
            deviation(B - 1)


def kernel(x, ctx_768, mask_BxS2_if1, L0_xattn_Wq, L0_xattn_Wk, L0_xattn_Wv, L0_xattn_Wo, L0_xattn_gamma,
           L0_xattn_beta):
    import concourse.bacc as bacc
    from concourse.bass_utils import run_bass_kernel_spmd

    def tiles(a):
        *lead, rows, cols = a.shape
        return np.ascontiguousarray(np.moveaxis(a.reshape(*lead, rows // P, P, cols), -3, -2))

    x, ctx, mask = np.asarray(x), np.asarray(ctx_768), np.asarray(mask_BxS2_if1)
    wq, wk, wv, wo = (np.asarray(w) for w in (L0_xattn_Wq, L0_xattn_Wk, L0_xattn_Wv, L0_xattn_Wo))
    ctxT = ctx.transpose(0, 2, 1)
    arrays = {
        "xT": tiles(x.transpose(0, 2, 1)),
        "x": tiles(x),
        "ctxT": tiles(np.concatenate([ctxT, ctxT[:, P:]], axis=1)),
        "ctx": tiles(ctx),
        "mask": np.ascontiguousarray(mask),
        "wqT": tiles(wq.T),
        "wkT": tiles(wk.T),
        "wvT": tiles(wv.T),
        "wo": tiles(wo),
        "gamma": np.asarray(L0_xattn_gamma).reshape(1, DI),
        "beta": np.asarray(L0_xattn_beta).reshape(1, DI),
    }
    nc = bacc.Bacc("TRN2", target_bir_lowering=False, num_devices=1)
    inputs = {f"in_{name}": a for name, a in arrays.items()}
    args = [nc.dram_tensor(name, a.shape, mybir.dt.from_np(a.dtype), kind="ExternalInput").ap()
            for name, a in inputs.items()]
    out = nc.dram_tensor("out", (B, P, QT, DI), F32, kind="ExternalOutput").ap()
    attention_kernel(nc, *args, out)
    result = run_bass_kernel_spmd(nc, [inputs], core_ids=[0])
    rows = result.results[0]["out"]
    return np.ascontiguousarray(rows.transpose(0, 2, 1, 3)).reshape(B, S, DI)
```

```python
from contextlib import ExitStack

import numpy as np

import concourse.bass as bass
from concourse import mybir

F32 = mybir.dt.float32
F32R = mybir.dt.float32r
I32 = mybir.dt.int32
ALU = mybir.AluOpType
ACT = mybir.ActivationFunctionType

P = 128
B = 8
S = 256
KV = 256
H = 8
D = 256
DI = 256
DL = 192
EPS = 1e-5
SCALE = 1.0 / D ** 0.5

UP = DL - P
PAIRS = H // 2
STEPS = B * PAIRS
QT = S // P
KT = KV // P
IT = DI // P
DT = D // P
PW = 2 * P + 2 * UP
MASKED = -3.0e38
LAG = 2
SQ = 32
SQUARES = KV // SQ
ROWS = P // SQ



def attention_kernel(nc, xT, x, ctxT, ctx, mask, wqT, wkT, wvT, wo, gamma, beta, out, scratch):
    es = ExitStack()
    with es:
        def sb(name, shape, dt=F32):
            return es.enter_context(nc.sbuf_tensor(name, shape, dt))

        def bank(name, shape):
            return es.enter_context(nc.psum_tensor(name, shape, F32))

        def sem(name):
            return es.enter_context(nc.semaphore(name))

        wq_raw = sb("wq_raw", [P, H * DT, DI])
        wk_raw = sb("wk_raw", [P, H * DT, DL])
        wv_raw = sb("wv_raw", [P, H * DT, DL])
        wo_raw = sb("wo_raw", [P, H * DT, DI])
        A_hi = sb("A_hi", [P, IT, PAIRS * PW], F32R)
        A_lo = sb("A_lo", [P, IT, PAIRS * PW], F32R)
        CL_hi = sb("CL_hi", [P, H, DI], F32R)
        CL_lo = sb("CL_lo", [P, H, DI], F32R)
        CU_hi = sb("CU_hi", [P, PAIRS, DI], F32R)
        CU_lo = sb("CU_lo", [P, PAIRS, DI], F32R)
        gamma_sb = sb("gamma_sb", [P, DI])
        beta_sb = sb("beta_sb", [P, DI])
        ident = sb("ident", [P, P])
        eps_col = sb("eps_col", [P, QT])
        power_col = sb("power_col", [P, QT])

        xT_raw = sb("xT_raw", [P, IT, S])
        xT_hi = sb("xT_hi", [P, IT, S], F32R)
        xT_lo = sb("xT_lo", [P, IT, S], F32R)
        ctxT_raw = sb("ctxT_raw", [P, 2, KV])
        ctxT_hi = sb("ctxT_hi", [P, 2, KV], F32R)
        ctxT_lo = sb("ctxT_lo", [P, 2, KV], F32R)
        ctx_raw = sb("ctx_raw", [P, KT, DL])
        ctxL_hi = sb("ctxL_hi", [P, KT, P], F32R)
        ctxL_lo = sb("ctxL_lo", [P, KT, P], F32R)
        ctxU = sb("ctxU", [P, KT, 3 * UP], F32R)
        mask_raw = sb("mask_raw", [P, KV], I32)
        mask_low = sb("mask_low", [P, KV])
        mask_bias = sb("mask_bias", [P, KV])
        x_res = sb("x_res", [P, QT, DI])

        gL_hi = sb("gL_hi", [P, 2, S], F32R)
        gL_lo = sb("gL_lo", [P, 2, S], F32R)
        gU = sb("gU", [P, 2, S], F32R)
        neg_scores = sb("neg_scores", [P, 2 * QT, KV])
        neg_max = sb("neg_max", [P, 2 * QT])
        probs = [sb(f"probs{n}", [P, 2 * QT, KV]) for n in range(2)]
        row_sum = sb("row_sum", [P, 2 * QT])
        inv_sum = sb("inv_sum", [P, 2 * QT])
        squares = sb("squares", [P, SQUARES, 2 * QT, SQ])
        pT_raw = [sb(f"pT_raw{n}", [P, KT, ROWS, 2 * QT, SQ]) for n in range(2)]
        pT_hi = sb("pT_hi", [P, KT, 2, S], F32R)
        pT_lo = sb("pT_lo", [P, KT, 2, S], F32R)
        tL_hi = sb("tL_hi", [P, 2, S], F32R)
        tL_lo = sb("tL_lo", [P, 2, S], F32R)
        tU_small = sb("tU_small", [P, S])
        tU = sb("tU", [P, S])
        tU_hi = sb("tU_hi", [P, S], F32R)
        tU_lo = sb("tU_lo", [P, S], F32R)

        y = sb("y", [P, QT, DI])
        y_scaled = sb("y_scaled", [P, QT, DI])
        y_out = sb("y_out", [P, QT, DI])
        stats = sb("stats", [P, QT, 6])
        mean_var = sb("mean_var", [P, QT, 2])
        var_eps = sb("var_eps", [P, QT])
        rstd = sb("rstd", [P, QT])

        score_bank = [bank("score_bank0", [P, QT, KV]), bank("score_bank1", [P, QT, KV])]
        tL_bank = bank("tL_bank", [P, 2, S])
        tU_bank = bank("tU_bank", [P, 2, S])
        gL_bank = bank("gL_bank", [P, 2, S])
        gU_bank = bank("gU_bank", [P, 2, S])
        out_bank = bank("out_bank", [P, QT, DI])
        spare_bank = bank("spare_bank", [P, 2, S])
        fold_banks = [spare_bank, out_bank, tL_bank, tU_bank]
        pT_banks = [gL_bank, gU_bank]

        def places(name, t):
            if not (isinstance(t, int) and t == STEPS - 1):
                return {"pT": (pT_hi[:], pT_lo[:]),
                        "tL": (tL_bank, tL_hi[:], tL_lo[:]),
                        "tU": (tU_bank, tU_hi[:], tU_lo[:])}[name]
            wide = [A[:, 0, 0:KT * 2 * S].rearrange("p (k hh s) -> p k hh s", k=KT, hh=2) for A in (A_hi, A_lo)]
            return {"pT": (wide[0], wide[1]),
                    "tL": (score_bank[0], xT_hi[:], xT_lo[:]),
                    "tU": (score_bank[1], gU[:, 0, :], gU[:, 1, :])}[name]

        def output(t, q):
            if q > 0 and isinstance(t, int) and t >= STEPS - PAIRS:
                return spare_bank[:].rearrange("p a c -> p (a c)")[:, 0:DI]
            return out_bank[:, q, :]

        q_head_in = [sem(f"q_head_in{h}") for h in range(2)]
        q_weights_in = [sem(f"q_weights_in{j}") for j in range(PAIRS)]
        o_weights_in = [sem(f"o_weights_in{j}") for j in range(PAIRS)]
        affine_in = sem("affine_in")
        xT_in = sem("xT_in")
        ctxT_in = sem("ctxT_in")
        ctx_in = sem("ctx_in")
        mask_in = sem("mask_in")
        x_res_in = sem("x_res_in")
        out_stored = sem("out_stored")
        constants = sem("constants")
        A_product = sem("A_product")
        A_hi_done = sem("A_hi_done")
        A_split = sem("A_split")
        C_product = sem("C_product")
        C_hi_done = sem("C_hi_done")
        C_split = sem("C_split")
        xT_hi_done = sem("xT_hi_done")
        xT_split = sem("xT_split")
        ctxT_hi_done = sem("ctxT_hi_done")
        ctxT_split = sem("ctxT_split")
        ctx_hi_done = sem("ctx_hi_done")
        ctx_split = sem("ctx_split")
        mask_lowered = sem("mask_lowered")
        mask_ready = sem("mask_ready")
        g_product = sem("g_product")
        g_hi_done = sem("g_hi_done")
        g_split = sem("g_split")
        scores_done = sem("scores_done")
        max_done = sem("max_done")
        exp_done = sem("exp_done")
        inv_done = sem("inv_done")
        probs_done = sem("probs_done")
        squares_done = sem("squares_done")
        squares_stored = sem("squares_stored")
        pT_in = [sem(f"pT_in{n}") for n in range(2)]
        pT_done = sem("pT_done")
        pT_hi_done = sem("pT_hi_done")
        pT_split = sem("pT_split")
        t_product = sem("t_product")
        t_hi_done = sem("t_hi_done")
        tU_small_done = sem("tU_small_done")
        tU_summed = sem("tU_summed")
        t_split = sem("t_split")
        out_product = sem("out_product")
        out_bank_read = sem("out_bank_read")
        stats_done = sem("stats_done")
        mean_done = sem("mean_done")
        var_eps_done = sem("var_eps_done")
        rstd_done = sem("rstd_done")
        y_scaled_done = sem("y_scaled_done")
        y_out_done = sem("y_out_done")

        waits_passed = sem("waits_passed")

        block = es.enter_context(nc.Block())

        def batch_of(src, b):
            if isinstance(b, int):
                return src[b]
            return src[bass.ds(b, 1)].rearrange("o p a c -> p (o a) c")

        @block.sync
        def _(sp):
            def load_xT(b):
                sp.dma_start(xT_raw[:], batch_of(xT, b)).then_inc(xT_in, 16)

            def load_ctxT(b):
                sp.dma_start(ctxT_raw[:], batch_of(ctxT, b)).then_inc(ctxT_in, 16)

            def load_ctx(b):
                sp.dma_start(ctx_raw[:], batch_of(ctx, b)).then_inc(ctx_in, 16)

            def load_x_res(b):
                sp.dma_start(x_res[:], batch_of(x, b)).then_inc(x_res_in, 16)

            def load_mask(b):
                src = mask[b:b + 1] if isinstance(b, int) else mask[bass.ds(b, 1)]
                sp.dma_start(mask_raw[:], src.broadcast_to((P, KV))).then_inc(mask_in, 16)

            def store_out(b):
                sp.wait_ge(y_out_done, QT * b + QT)
                sp.dma_start(batch_of(out, b), y_out[:]).then_inc(out_stored, 16)

            sp.sem_inc(out_stored, 16)
            for j in range(PAIRS):
                if j > 0:
                    tiles = slice(2 * j * DT, 2 * (j + 1) * DT)
                    sp.dma_start(wk_raw[:, tiles], wkT[:, tiles]).then_inc(q_weights_in[j], 16)
                    sp.dma_start(wq_raw[:, tiles], wqT[:, tiles]).then_inc(q_weights_in[j], 16)
                else:
                    for h in range(2):
                        tiles = slice(h * DT, (h + 1) * DT)
                        sp.dma_start(wk_raw[:, tiles], wkT[:, tiles]).then_inc(q_head_in[h], 16)
                    load_xT(0)
            load_ctxT(0)
            load_mask(0)
            load_ctx(0)
            for j in range(PAIRS):
                tiles = slice(2 * j * DT, 2 * (j + 1) * DT)
                sp.dma_start(wv_raw[:, tiles], wvT[:, tiles]).then_inc(o_weights_in[j], 16)
                sp.dma_start(wo_raw[:, tiles], wo[:, tiles]).then_inc(o_weights_in[j], 16)
            load_x_res(0)
            sp.dma_start(gamma_sb[:], gamma.broadcast_to((P, DI))).then_inc(affine_in, 16)
            sp.dma_start(beta_sb[:], beta.broadcast_to((P, DI))).then_inc(affine_in, 16)

            def load_ahead(b):
                sp.wait_ge(xT_split, b)
                load_xT(b)
                sp.wait_ge(ctxT_split, b)
                load_ctxT(b)
                sp.wait_ge(mask_lowered, b)
                load_mask(b)

            def load_ctx_ahead(b):
                sp.wait_ge(ctx_split, 2 * b)
                load_ctx(b)

            def load_residual(b):
                sp.wait_ge(out_bank_read, b + 1)
                load_x_res(b)

            def carry_squares(t, j, raw_free=True):
                sp.wait_ge(squares_done, 2 * QT * t + 2 * QT)
                sp.dma_start(scratch[j].rearrange("i c k jj r -> (i c) (k jj r)"),
                             squares[:].rearrange("p s n r -> p (s n r)")).then_inc(squares_stored, 16)
                sp.wait_ge(squares_stored, 16 * t + 16)
                if raw_free:
                    sp.wait_ge(pT_split, 2 * (t - 2) + 2)
                for jj in range(ROWS):
                    sp.dma_start(pT_raw[j % 2][SQ * jj:SQ * (jj + 1)].rearrange("c k i n r -> c k i (n r)"),
                                 scratch[j][:, :, :, jj, :].rearrange("i c k r -> c k i r")).then_inc(pT_in[j % 2], 16)

            load_ahead(1)
            carry_squares(0, 0, raw_free=False)
            load_ctx_ahead(1)
            carry_squares(1, 1, raw_free=False)
            for t in range(2, PAIRS + 1):
                carry_squares(t, t % PAIRS)
            with sp.Fori(1, B - 1) as b:
                load_ahead(b + 1)
                carry_squares(PAIRS * b + 1, 1)
                load_ctx_ahead(b + 1)
                load_residual(b)
                carry_squares(PAIRS * b + 2, 2)
                store_out(b - 1)
                carry_squares(PAIRS * b + 3, 3)
                carry_squares(PAIRS * b + 4, 0)
            carry_squares(STEPS - 3, 1)
            load_residual(B - 1)
            store_out(B - 2)
            for q in range(QT):
                sp.wait_ge(y_out_done, QT * (B - 1) + 1 + q)
                sp.dma_start(out[B - 1][:, q, :], y_out[:, q, :]).then_inc(out_stored, 16)
            sp.wait_ge(out_stored, 16 * (B + QT))

        @block.tensor
        def _(pe):
            def split_products(into, pairs, first=True, last=True, shared=False):
                for n, (stationary, moving) in enumerate(pairs):
                    ins = nc.tensor.matmul(into, stationary, moving, start=first and n == 0,
                                           stop=last and n == len(pairs) - 1, skip_group_check=shared)
                return ins

            def fold_A(h):
                if h < 2:
                    pe.wait_ge(q_head_in[h], 32)
                elif h % 2 == 0:
                    pe.wait_ge(q_weights_in[h // 2], 32)
                if h >= len(fold_banks):
                    pe.wait_ge(A_split, 2 * (h - len(fold_banks)) + 2)
                dst = fold_banks[h % len(fold_banks)][:].rearrange("p a c -> p (a c)")
                for i in range(IT):
                    for d in range(DT):
                        ins = nc.tensor.matmul(dst[:, i * DL:(i + 1) * DL],
                                               wq_raw[:, h * DT + d, i * P:(i + 1) * P],
                                               wk_raw[:, h * DT + d, :], start=d == 0, stop=d == DT - 1)
                ins.then_inc(A_product, 1)

            def fold_C(j):
                pe.wait_ge(o_weights_in[j], 32)
                if j == 0:
                    pe.wait_ge(A_split, 2 * H)
                if j >= 2:
                    pe.wait_ge(C_split, 2 * (j - 2) + 2)
                lower, upper = fold_banks[2 * (j % 2)], fold_banks[2 * (j % 2) + 1]
                for hh in range(2):
                    h = 2 * j + hh
                    for d in range(DT):
                        ins = nc.tensor.matmul(lower[:, hh, :], wv_raw[:, h * DT + d, 0:P],
                                               wo_raw[:, h * DT + d, :], start=d == 0, stop=d == DT - 1)
                ins.then_inc(C_product, 1)
                for hh in range(2):
                    h = 2 * j + hh
                    for d in range(DT):
                        ins = nc.tensor.matmul(upper[hh * UP:(hh + 1) * UP, 0, :],
                                               wv_raw[:, h * DT + d, P:DL],
                                               wo_raw[:, h * DT + d, :], start=d == 0, stop=d == DT - 1)
                ins.then_inc(C_product, 1)

            def query_products(t, j, b):
                if j == 0:
                    pe.wait_ge(xT_split, b + 1)
                col = j * PW

                def tile(into, at):
                    pairs = []
                    for i in range(IT):
                        hi, lo = A_hi[:, i, at:at + P], A_lo[:, i, at:at + P]
                        pairs += [(hi, xT_hi[:, i, :]), (hi, xT_lo[:, i, :]), (lo, xT_hi[:, i, :])]
                    return split_products(into, pairs)

                tile(gU_bank[:, 0, :], col + 2 * P).then_inc(g_product, 1)
                tile(gL_bank[:, 0, :], col)
                tile(gL_bank[:, 1, :], col + P).then_inc(g_product, 1)

            def scores(t, j, b):
                if j == 0:
                    pe.wait_ge(ctxT_split, b + 1)
                for hh in range(2):
                    if hh == 0:
                        pe.wait_ge(g_hi_done, 3 * t + 3)
                        pe.wait_ge(g_split, 3 * t + 2)
                    for q in range(QT):
                        rows = slice(q * P, (q + 1) * P)
                        hi, lo, up = gL_hi[:, hh, rows], gL_lo[:, hh, rows], gU[:, hh, rows]
                        split_products(score_bank[hh][:, q, :],
                                       [(up, ctxT_hi[:, 1, :]), (up, ctxT_lo[:, 1, :]),
                                        (hi, ctxT_hi[:, 0, :]), (hi, ctxT_lo[:, 0, :])], last=False)
                        if hh == 0 and q == 0:
                            pe.wait_ge(g_split, 3 * t + 3)
                        ins = split_products(score_bank[hh][:, q, :], [(lo, ctxT_hi[:, 0, :])], first=False)
                    ins.then_inc(scores_done, 1)

            def transposes(t):
                for hh in range(2):
                    pe.wait_ge(probs_done, 2 * t + 1 + hh)
                    if t == STEPS - 1:
                        pe.wait_ge(pT_split, 2 * t - 1 + hh)
                    for k in range(KT):
                        for q in range(QT):
                            ins = nc.tensor.transpose(pT_banks[hh][:, k, q * P:(q + 1) * P],
                                                      probs[t % 2][:, hh * QT + q, k * P:(k + 1) * P],
                                                      ident[:])
                    ins.then_inc(pT_done, 1)

            def context_products(t, j, b):
                if j == 0:
                    pe.wait_ge(C_split, 2 * PAIRS)
                    pe.wait_ge(ctx_split, 2 * b + 2)
                (hi, lo), tL, tU = places("pT", t), places("tL", t)[0], places("tU", t)[0]
                pe.wait_ge(pT_hi_done, 2 * t + 2)
                split_products(tL[:], [(part[:, k, :], hi[:, k]) for k in range(KT)
                                            for part in (ctxL_hi, ctxL_lo)], last=False)
                hi_lo = [ctxU[:, :, 0:2 * UP], ctxU[:, :, UP:3 * UP]]
                for hh in range(2):
                    split_products(tU[:, hh, :], [(hi_lo[hh][:, k], hi[:, k, hh]) for k in range(KT)],
                                   first=hh == 0, last=False, shared=True)
                by_squares = not (isinstance(t, int) and t >= STEPS - 2)
                for k in range(KT):
                    pe.wait_ge(pT_split, 2 * t + (k + 1 if by_squares else 2))
                    end = k == KT - 1
                    lower = split_products(tL[:], [(ctxL_hi[:, k, :], lo[:, k])], first=False, last=end)
                    if end:
                        lower.then_inc(t_product, 1)
                    for hh in range(2):
                        upper = split_products(tU[:, hh, :], [(hi_lo[hh][:, k], lo[:, k, hh])],
                                               first=False, last=end, shared=True)
                upper.then_inc(t_product, 1)

            def output_products(t, j, b):
                (_, L_hi, L_lo), (_, U_hi, U_lo) = places("tL", t), places("tU", t)

                def lower(q):
                    rows = slice(q * P, (q + 1) * P)
                    pairs = []
                    for hh in range(2):
                        hi, lo, h = L_hi[:, hh, rows], L_lo[:, hh, rows], 2 * j + hh
                        pairs += [(hi, CL_hi[:, h]), (hi, CL_lo[:, h]), (lo, CL_hi[:, h])]
                    own = isinstance(t, int) and t >= STEPS - PAIRS
                    split_products(output(t, q), pairs, first=j == 0 and (q == 0 or own), last=False, shared=True)

                def upper(q):
                    rows = slice(q * P, (q + 1) * P)
                    hi, lo = U_hi[:, rows], U_lo[:, rows]
                    pairs = [(hi, CU_hi[:, j]), (hi, CU_lo[:, j]), (lo, CU_hi[:, j])]
                    return split_products(output(t, q), pairs, first=False, last=j == PAIRS - 1, shared=True)

                if j == 0:
                    pe.wait_ge(out_bank_read, b + 1)
                pe.wait_ge(t_split, 2 * t + 1)
                lower(0)
                if isinstance(t, int) and t == STEPS - 1:
                    pe.wait_ge(t_split, 2 * t + 2)
                    upper(0).then_inc(out_product, 1)
                    lower(1)
                    upper(1).then_inc(out_product, 1)
                    return
                lower(1)
                pe.wait_ge(t_split, 2 * t + 2)
                upper(0)
                upper(1).then_inc(out_product, 1)

            def step(t, j, b):
                jb, bb = (j - LAG) % PAIRS, b - 1 if j < LAG else b
                ja, ba = (j + 1) % PAIRS, b + 1 if j == PAIRS - 1 else b
                scores(t, j, b)
                context_products(t - LAG, jb, bb)
                query_products(t + 1, ja, ba)
                output_products(t - LAG, jb, bb)

            for h in range(H - 2):
                fold_A(h)
            pe.wait_ge(A_split, 4)
            query_products(0, 0, 0)
            for h in range(H - 2, H):
                fold_A(h)
            scores(0, 0, 0)
            fold_C(0)
            query_products(1, 1, 0)
            fold_C(1)
            scores(1, 1, 0)
            fold_C(2)
            query_products(2, 2, 0)
            fold_C(3)
            with pe.Fori(0, B - 1) as b:
                step(PAIRS * b + 2, 2, b)
                step(PAIRS * b + 3, 3, b)
                step(PAIRS * b + 4, 0, b + 1)
                step(PAIRS * b + 5, 1, b + 1)
            step(STEPS - 2, 2, B - 1)
            scores(STEPS - 1, 3, B - 1)
            context_products(STEPS - 3, 1, B - 1)
            pe.wait_ge(constants, 3)
            transposes(STEPS - 2)
            output_products(STEPS - 3, 1, B - 1)
            transposes(STEPS - 1)
            context_products(STEPS - 2, 2, B - 1)
            context_products(STEPS - 1, 3, B - 1)
            output_products(STEPS - 2, 2, B - 1)
            output_products(STEPS - 1, 3, B - 1)

        @block.scalar
        def _(act):
            def hi_part(dst, src):
                return nc.scalar.activation(dst, src, ACT.Copy)

            def A_hi_part(h):
                act.wait_ge(A_product, h + 1)
                src = fold_banks[h % len(fold_banks)][:].rearrange("p a c -> p (a c)")[:, 0:IT * DL] \
                    .rearrange("p (i f) -> p i f", i=IT)
                low = (h // 2) * PW + (h % 2) * P
                up = (h // 2) * PW + 2 * P + (h % 2) * UP
                hi_part(A_hi[:, :, low:low + P], src[:, :, 0:P]).then_inc(A_hi_done, 1)
                hi_part(A_hi[:, :, up:up + UP], src[:, :, P:DL]).then_inc(A_hi_done, 1)

            def C_hi_part(j):
                lower, upper = fold_banks[2 * (j % 2)], fold_banks[2 * (j % 2) + 1]
                act.wait_ge(C_product, 2 * j + 1)
                hi_part(CL_hi[:, 2 * j:2 * j + 2, :], lower[:]).then_inc(C_hi_done, 1)
                act.wait_ge(C_product, 2 * j + 2)
                hi_part(CU_hi[:, j, :], upper[:, 0, :]).then_inc(C_hi_done, 1)

            def ctxT_hi_part(b):
                act.wait_ge(ctxT_in, 16 * b + 16)
                hi_part(ctxT_hi[:], ctxT_raw[:]).then_inc(ctxT_hi_done, 1)

            def gU_hi_part(t):
                act.wait_ge(g_product, 2 * t + 1)
                hi_part(gU[0:UP, 0, :], gU_bank[0:UP, 0, :]).then_inc(g_hi_done, 1)
                hi_part(gU[UP:P, 1, :], gU_bank[UP:P, 0, :]).then_inc(g_hi_done, 1)

            def gL_hi_part(t):
                act.wait_ge(g_product, 2 * t + 2)
                hi_part(gL_hi[:], gL_bank[:]).then_inc(g_hi_done, 1)

            def exponentials(t, j):
                if not (isinstance(t, int) and t < 2):
                    act.wait_ge(squares_done, 2 * QT * (t - 1))
                for n in range(2 * QT):
                    act.wait_ge(max_done, 4 * t + 1 + n)
                    nc.scalar.activation(probs[j % 2][:, n, :], neg_scores[:, n, :], ACT.Exp,
                                         bias=neg_max[:, n:n + 1], scale=-1.0,
                                         accum_out=row_sum[:, n:n + 1]).then_inc(exp_done, 1)

            def xT_hi_part(b):
                act.wait_ge(xT_in, 16 * b + 16)
                hi_part(xT_hi[:], xT_raw[:]).then_inc(xT_hi_done, 1)

            def pT_hi_part(t, j):
                if isinstance(t, int) and t >= STEPS - 2:
                    for hh in range(2):
                        act.wait_ge(pT_done, 2 * (t - STEPS + 2) + 1 + hh)
                        hi_part(places("pT", t)[0][:, :, hh, :], pT_banks[hh][:]).then_inc(pT_hi_done, 1)
                    return
                act.wait_ge(pT_in[j % 2], 16 * ROWS // 2 * (t - j % 2) + 16 * ROWS)
                for k in range(KT):
                    hi_part(pT_hi[:, k].rearrange("p hh (q i r) -> p (hh q) i r", q=QT, i=ROWS),
                            pT_raw[j % 2][:, k].rearrange("p i n r -> p n i r")).then_inc(pT_hi_done, 1)

            def ctx_hi_part(b):
                act.wait_ge(ctx_in, 16 * b + 16)
                lower, upper = ctx_raw[:, :, 0:P], ctx_raw[:, :, P:DL]
                hi_part(ctxL_hi[:], lower).then_inc(ctx_hi_done, 1)
                hi_part(ctxU[:, :, 0:UP], upper).then_inc(ctx_hi_done, 1)
                hi_part(ctxU[:, :, 2 * UP:3 * UP], upper).then_inc(ctx_hi_done, 1)

            def t_hi_part(t):
                act.wait_ge(t_product, 2 * t + 1)
                L_bank, L_hi, _ = places("tL", t)
                hi_part(L_hi, L_bank[:]).then_inc(t_hi_done, 1)
                act.wait_ge(t_product, 2 * t + 2)
                U_bank = places("tU", t)[0]
                nc.scalar.activation(tU_small[0:UP, :], U_bank[UP:P, 0, :], ACT.Copy).then_inc(tU_small_done, 1)
                nc.scalar.activation(tU_small[UP:P, :], U_bank[0:UP, 1, :], ACT.Copy).then_inc(tU_small_done, 1)

            def tU_hi_part(t):
                act.wait_ge(tU_summed, 2 * t + 2)
                hi_part(places("tU", t)[1], tU[:]).then_inc(t_hi_done, 1)

            def step(t, j, b, before=True, after=True):
                exponentials(t, j)
                if j == PAIRS - 1 and after:
                    ctxT_hi_part(b + 1)
                if before:
                    t_hi_part(t - LAG)
                if after:
                    gU_hi_part(t + 1)
                if before:
                    tU_hi_part(t - LAG)
                if after:
                    gL_hi_part(t + 1)
                if j == 2 and after and not (isinstance(b, int) and b == B - 1):
                    xT_hi_part(b + 1)
                if j == 1:
                    ctx_hi_part(b)
                pT_hi_part(t - 1, (j - 1) % PAIRS)

            for h in range(2):
                tiles = slice(h * DT, (h + 1) * DT)
                act.dma_start(wq_raw[:, tiles], wqT[:, tiles]).then_inc(q_head_in[h], 16)
            A_hi_part(0)
            A_hi_part(1)
            xT_hi_part(0)
            for h in range(2, H - 2):
                A_hi_part(h)
            gU_hi_part(0)
            gL_hi_part(0)
            ctxT_hi_part(0)
            for h in range(H - 2, H):
                A_hi_part(h)
            exponentials(0, 0)
            C_hi_part(0)
            gU_hi_part(1)
            gL_hi_part(1)
            C_hi_part(1)
            exponentials(1, 1)
            ctx_hi_part(0)
            C_hi_part(2)
            gU_hi_part(2)
            gL_hi_part(2)
            C_hi_part(3)
            pT_hi_part(0, 0)
            with act.Fori(0, B - 1) as b:
                step(PAIRS * b + 2, 2, b)
                step(PAIRS * b + 3, 3, b)
                step(PAIRS * b + 4, 0, b + 1)
                step(PAIRS * b + 5, 1, b + 1)
            step(STEPS - 2, 2, B - 1)
            exponentials(STEPS - 1, 3)
            t_hi_part(STEPS - 3)
            tU_hi_part(STEPS - 3)
            for t in (STEPS - 2, STEPS - 1):
                pT_hi_part(t, t % PAIRS)
            for t in (STEPS - 2, STEPS - 1):
                t_hi_part(t)
                tU_hi_part(t)

        @block.vector
        def _(dve):
            def waited():
                dve.sem_inc(waits_passed, 1)

            def lo_part(dst, whole, hi):
                return nc.vector.tensor_tensor(dst, whole, hi.bitcast(F32), ALU.subtract)

            def A_lo_part(h):
                src = fold_banks[h % len(fold_banks)][:].rearrange("p a c -> p (a c)")[:, 0:IT * DL] \
                    .rearrange("p (i f) -> p i f", i=IT)
                low = (h // 2) * PW + (h % 2) * P
                up = (h // 2) * PW + 2 * P + (h % 2) * UP
                dve.wait_ge(A_hi_done, 2 * h + 2)
                lo_part(A_lo[:, :, low:low + P], src[:, :, 0:P], A_hi[:, :, low:low + P]).then_inc(A_split, 1)
                lo_part(A_lo[:, :, up:up + UP], src[:, :, P:DL], A_hi[:, :, up:up + UP]).then_inc(A_split, 1)

            def C_lo_part(j):
                lower, upper = fold_banks[2 * (j % 2)], fold_banks[2 * (j % 2) + 1]
                dve.wait_ge(C_hi_done, 2 * j + 1)
                lo_part(CL_lo[:, 2 * j:2 * j + 2, :], lower[:], CL_hi[:, 2 * j:2 * j + 2, :]).then_inc(C_split, 1)
                dve.wait_ge(C_hi_done, 2 * j + 2)
                lo_part(CU_lo[:, j, :], upper[:, 0, :], CU_hi[:, j, :]).then_inc(C_split, 1)

            def lower_mask(b):
                dve.wait_ge(mask_in, 16 * b + 16)
                nc.vector.tensor_scalar(mask_low[:], mask_raw[:], 0, MASKED, ALU.is_equal,
                                        ALU.mult).then_inc(mask_lowered, 1)

            def finish_mask(b):
                dve.wait_ge(mask_lowered, b + 1)
                nc.vector.tensor_scalar(mask_bias[:], mask_low[:], 4.0, None, ALU.mult).then_inc(mask_ready, 1)

            def gU_lo_part(t):
                dve.wait_ge(g_hi_done, 3 * t + 2)
                lo_part(gU[UP:P, 0, :], gU_bank[0:UP, 0, :], gU[0:UP, 0, :]).then_inc(g_split, 1)
                lo_part(gU[0:UP, 1, :], gU_bank[UP:P, 0, :], gU[UP:P, 1, :]).then_inc(g_split, 1)

            def gL_lo_part(t):
                dve.wait_ge(g_hi_done, 3 * t + 3)
                lo_part(gL_lo[:], gL_bank[:], gL_hi[:]).then_inc(g_split, 1)

            def maxima(t, b):
                for hh in range(2):
                    dve.wait_ge(mask_ready, b + 1)
                    dve.wait_ge(scores_done, 2 * t + 1 + hh)
                    waited()
                    for q in range(QT):
                        n = hh * QT + q
                        nc.vector.tensor_tensor_reduce(
                            out=neg_scores[:, n, :], in0=score_bank[hh][:, q, :], in1=mask_bias[:],
                            scale=-SCALE, scalar=3.0e38, op0=ALU.add, op1=ALU.min,
                            accum_out=neg_max[:, n:n + 1]).then_inc(max_done, 1)

            def inverse_sum(t, hh):
                if isinstance(t, int) and t == STEPS - 1:
                    dve.wait_ge(probs_done, 2 * t - 1 + hh)
                dve.wait_ge(exp_done, 4 * t + QT * (hh + 1))
                nc.vector.reciprocal(inv_sum[:, QT * hh:QT * hh + QT],
                                     row_sum[:, QT * hh:QT * hh + QT]).then_inc(inv_done, 1)

            def transpose_squares(t, j, hh):
                if hh == 0 and not (isinstance(t, int) and t == 0):
                    dve.wait_ge(squares_stored, 16 * t)
                dve.wait_ge(probs_done, 2 * t + 1 + hh)
                for n in range(QT * hh, QT * hh + QT):
                    nc.vector.transpose(squares[:, :, n, :],
                                        probs[j % 2][:, n, :].rearrange("p (s c) -> p s c", c=SQ)) \
                        .then_inc(squares_done, 1)

            def pT_lo_part(t):
                for hh in range(2):
                    dve.wait_ge(pT_hi_done, 2 * t + 1 + hh)
                    hi, lo = places("pT", t)
                    lo_part(lo[:, :, hh, :], pT_banks[hh][:], hi[:, :, hh, :]).then_inc(pT_split, 1)

            def t_lo_part_lower(t):
                dve.wait_ge(t_hi_done, 2 * t + 1)
                L_bank, L_hi, L_lo = places("tL", t)
                lo_part(L_lo, L_bank[:], L_hi).then_inc(t_split, 1)

            def tU_sum(t):
                if isinstance(t, int) and t == STEPS - 1:
                    dve.wait_ge(t_split, 2 * t)
                dve.wait_ge(tU_small_done, 2 * t + 2)
                for hh, part in enumerate((slice(0, UP), slice(UP, P))):
                    nc.vector.tensor_tensor(tU[part, :], places("tU", t)[0][part, hh, :], tU_small[part, :],
                                            ALU.add).then_inc(tU_summed, 1)

            def t_lo_part_upper(t):
                dve.wait_ge(t_hi_done, 2 * t + 2)
                _, U_hi, U_lo = places("tU", t)
                lo_part(U_lo, tU[:], U_hi).then_inc(t_split, 1)

            def add_residual(b):
                dve.wait_ge(x_res_in, 16 * b + 16)
                dve.wait_ge(out_product, PAIRS * b + PAIRS)
                nc.vector.tensor_tensor(y[:], out_bank[:], x_res[:], ALU.add).then_inc(out_bank_read, 1)

            def statistics(b):
                dve.wait_ge(out_bank_read, b + 2)
                for q in range(QT):
                    nc.vector.bn_stats(stats[:, q, :], y[:, q, :]).then_inc(stats_done, 1)
                for q in range(QT):
                    dve.wait_ge(stats_done, QT * b + q + 1)
                    waited()
                    nc.vector.bn_aggr(mean_var[:, q, :], stats[:, q, :]).then_inc(mean_done, 1)

            def centre_tile(q):
                nc.vector.scalar_tensor_tensor(
                    y_scaled[:, q, :], y[:, q, :], mean_var[:, q, 0:1], gamma_sb[:],
                    ALU.subtract, ALU.mult).then_inc(y_scaled_done, 1)

            def normalise_tile(b, q):
                dve.wait_ge(y_scaled_done, QT * b + q + 1)
                nc.vector.scalar_tensor_tensor(
                    y_out[:, q, :], y_scaled[:, q, :], rstd[:, q:q + 1], beta_sb[:],
                    ALU.mult, ALU.add).then_inc(y_out_done, 1)

            def centre(b):
                for q in range(QT):
                    if q == 0:
                        dve.wait_ge(mean_done, QT * b + QT)
                    centre_tile(q)

            def normalise(b):
                dve.wait_ge(rstd_done, b + 1)
                dve.wait_ge(out_stored, 16 * b + 16)
                for q in range(QT):
                    normalise_tile(b, q)

            def step(t, j, b, before=True, after=True, ends=None):
                by_squares = not (isinstance(t, int) and t >= STEPS - 2)
                if ends is not None and j == 2:
                    add_residual(ends)
                maxima(t, b)
                if ends is not None and j == 2:
                    statistics(ends)
                inverse_sum(t, 0)
                if ends is not None and j == 3:
                    centre(ends)
                inverse_sum(t, 1)
                if ends is not None and j == 3:
                    normalise(ends)
                if j == 3 and after:
                    finish_mask(b + 1)
                if before:
                    t_lo_part_lower(t - LAG)
                    tU_sum(t - LAG)
                if after:
                    gU_lo_part(t + 1)
                if before:
                    t_lo_part_upper(t - LAG)
                if by_squares:
                    transpose_squares(t, j, 0)
                if after:
                    gL_lo_part(t + 1)
                if by_squares:
                    transpose_squares(t, j, 1)
                if j == 2 and not (isinstance(b, int) and b == B - 1):
                    lower_mask(b + 1)

            dve.sem_inc(out_bank_read, 1)
            for h in range(H - 2):
                A_lo_part(h)
            gU_lo_part(0)
            gL_lo_part(0)
            for h in range(H - 2, H):
                A_lo_part(h)
            lower_mask(0)
            finish_mask(0)
            maxima(0, 0)
            inverse_sum(0, 0)
            inverse_sum(0, 1)
            C_lo_part(0)
            gU_lo_part(1)
            gL_lo_part(1)
            C_lo_part(1)
            transpose_squares(0, 0, 0)
            transpose_squares(0, 0, 1)
            maxima(1, 0)
            inverse_sum(1, 0)
            inverse_sum(1, 1)
            C_lo_part(2)
            gU_lo_part(2)
            gL_lo_part(2)
            transpose_squares(1, 1, 0)
            transpose_squares(1, 1, 1)
            C_lo_part(3)
            dve.wait_ge(affine_in, 32)
            for t in range(2, PAIRS + 2):
                step(t, t % PAIRS, t // PAIRS)
            with dve.Fori(1, B - 1) as b:
                step(PAIRS * b + 2, 2, b, ends=b - 1)
                step(PAIRS * b + 3, 3, b, ends=b - 1)
                step(PAIRS * b + 4, 0, b + 1)
                step(PAIRS * b + 5, 1, b + 1)
            step(STEPS - 2, 2, B - 1, ends=B - 2)
            step(STEPS - 1, 3, B - 1, after=False, ends=B - 2)
            for t in (STEPS - 2, STEPS - 1):
                pT_lo_part(t)
            for t in (STEPS - 2, STEPS - 1):
                t_lo_part_lower(t)
                tU_sum(t)
                t_lo_part_upper(t)
            for q in range(QT):
                dve.wait_ge(out_product, STEPS + q)
                if q == 0:
                    dve.wait_ge(x_res_in, 16 * B)
                nc.vector.tensor_tensor(y[:, q, :], output(STEPS - 1, q), x_res[:, q, :], ALU.add) \
                    .then_inc(out_bank_read, 1)
                dve.wait_ge(out_bank_read, B + 1 + q)
                nc.vector.bn_stats(stats[:, q, :], y[:, q, :]).then_inc(stats_done, 1)
                dve.wait_ge(stats_done, QT * (B - 1) + 1 + q)
                nc.vector.bn_aggr(mean_var[:, q, :], stats[:, q, :]).then_inc(mean_done, 1)
                dve.wait_ge(mean_done, QT * (B - 1) + 1 + q)
                centre_tile(q)
            dve.wait_ge(out_stored, 16 * B)
            for q in range(QT):
                dve.wait_ge(rstd_done, B + q)
                normalise_tile(B - 1, q)

        @block.gpsimd
        def _(pool):
            nc.gpsimd.memset(ident[:], 0.0).then_inc(constants, 1)
            nc.gpsimd.memset(eps_col[:], EPS)
            nc.gpsimd.memset(power_col[:], -0.5).then_inc(constants, 1)
            pool.wait_ge(constants, 2)
            nc.gpsimd.affine_select(out=ident[:], in_=ident[:], compare_op=ALU.not_equal, fill=1.0, base=0,
                                    pattern=[[-1, P]], channel_multiplier=1).then_inc(constants, 1)

            def normalise_probs(t, j):
                for hh in range(2):
                    rows = slice(QT * hh, QT * hh + QT)
                    inv = inv_sum[:, rows].rearrange("p (n o) -> p n o", o=1).broadcast_to((P, QT, KV))
                    pool.wait_ge(inv_done, 2 * t + 1 + hh)
                    nc.gpsimd.tensor_tensor(probs[j % 2][:, rows, :], probs[j % 2][:, rows, :], inv, ALU.mult) \
                        .then_inc(probs_done, 1)

            def deviation(b):
                pool.wait_ge(mean_done, QT * b + QT)
                nc.gpsimd.tensor_tensor(var_eps[:], mean_var[:, :, 1], eps_col[:], ALU.add).then_inc(var_eps_done, 1)
                pool.wait_ge(var_eps_done, b + 1)
                nc.gpsimd.tensor_tensor(rstd[:], var_eps[:], power_col[:], ALU.pow).then_inc(rstd_done, 1)

            def lo_part(dst, whole, hi):
                return nc.gpsimd.tensor_tensor(dst, whole, hi.bitcast(F32), ALU.subtract)

            def xT_lo_part(b):
                pool.wait_ge(xT_hi_done, b + 1)
                lo_part(xT_lo[:], xT_raw[:], xT_hi[:]).then_inc(xT_split, 1)

            def pT_lo_part(t, j):
                for k in range(KT):
                    pool.wait_ge(pT_hi_done, 2 * t + 1 + k)
                    nc.gpsimd.tensor_tensor(
                        pT_lo[:, k].rearrange("p hh (q i r) -> p (hh q) i r", q=QT, i=ROWS),
                        pT_raw[j % 2][:, k].rearrange("p i n r -> p n i r"),
                        pT_hi[:, k].rearrange("p hh (q i r) -> p (hh q) i r", q=QT, i=ROWS).bitcast(F32),
                        ALU.subtract).then_inc(pT_split, 1)

            def ctxT_lo_part(b):
                pool.wait_ge(ctxT_hi_done, b + 1)
                lo_part(ctxT_lo[:], ctxT_raw[:], ctxT_hi[:]).then_inc(ctxT_split, 1)

            def ctx_lo_part(b):
                pool.wait_ge(ctx_hi_done, 3 * b + 3)
                lower, upper = ctx_raw[:, :, 0:P], ctx_raw[:, :, P:DL]
                lo_part(ctxL_lo[:], lower, ctxL_hi[:]).then_inc(ctx_split, 1)
                lo_part(ctxU[:, :, UP:2 * UP], upper, ctxU[:, :, 0:UP]).then_inc(ctx_split, 1)

            def step(t, j, b, ends=None):
                normalise_probs(t, j)
                if j == PAIRS - 1 and not (isinstance(b, int) and b == B - 1):
                    ctxT_lo_part(b + 1)
                if j == 1:
                    ctx_lo_part(b)
                if ends is not None:
                    deviation(ends)
                if j == 2 and not (isinstance(b, int) and b == B - 1):
                    xT_lo_part(b + 1)
                pT_lo_part(t - 1, (j - 1) % PAIRS)

            xT_lo_part(0)
            ctxT_lo_part(0)
            normalise_probs(0, 0)
            for t in range(1, PAIRS + 2):
                step(t, t % PAIRS, t // PAIRS)
            with pool.Fori(1, B - 1) as b:
                step(PAIRS * b + 2, 2, b, ends=b - 1)
                step(PAIRS * b + 3, 3, b)
                step(PAIRS * b + 4, 0, b + 1)
                step(PAIRS * b + 5, 1, b + 1)
            step(STEPS - 2, 2, B - 1, ends=B - 2)
            normalise_probs(STEPS - 1, 3)
            for q in range(QT):
                col = slice(q, q + 1)
                pool.wait_ge(mean_done, QT * (B - 1) + 1 + q)
                nc.gpsimd.tensor_tensor(var_eps[:, col], mean_var[:, q, 1:2], eps_col[:, col], ALU.add) \
                    .then_inc(var_eps_done, 1)
                pool.wait_ge(var_eps_done, B + q)
                nc.gpsimd.tensor_tensor(rstd[:, col], var_eps[:, col], power_col[:, col], ALU.pow) \
                    .then_inc(rstd_done, 1)


def kernel(x, ctx_768, mask_BxS2_if1, L0_xattn_Wq, L0_xattn_Wk, L0_xattn_Wv, L0_xattn_Wo, L0_xattn_gamma,
           L0_xattn_beta):
    import concourse.bacc as bacc
    from concourse.bass_utils import run_bass_kernel_spmd

    def tiles(a):
        *lead, rows, cols = a.shape
        return np.ascontiguousarray(np.moveaxis(a.reshape(*lead, rows // P, P, cols), -3, -2))

    x, ctx, mask = np.asarray(x), np.asarray(ctx_768), np.asarray(mask_BxS2_if1)
    wq, wk, wv, wo = (np.asarray(w) for w in (L0_xattn_Wq, L0_xattn_Wk, L0_xattn_Wv, L0_xattn_Wo))
    ctxT = ctx.transpose(0, 2, 1)
    arrays = {
        "xT": tiles(x.transpose(0, 2, 1)),
        "x": tiles(x),
        "ctxT": tiles(np.concatenate([ctxT, ctxT[:, P:]], axis=1)),
        "ctx": tiles(ctx),
        "mask": np.ascontiguousarray(mask),
        "wqT": tiles(wq.T),
        "wkT": tiles(wk.T),
        "wvT": tiles(wv.T),
        "wo": tiles(wo),
        "gamma": np.asarray(L0_xattn_gamma).reshape(1, DI),
        "beta": np.asarray(L0_xattn_beta).reshape(1, DI),
    }
    nc = bacc.Bacc("TRN2", target_bir_lowering=False, num_devices=1)
    inputs = {f"in_{name}": a for name, a in arrays.items()}
    args = [nc.dram_tensor(name, a.shape, mybir.dt.from_np(a.dtype), kind="ExternalInput").ap()
            for name, a in inputs.items()]
    out = nc.dram_tensor("out", (B, P, QT, DI), F32, kind="ExternalOutput").ap()
    scratch = nc.dram_tensor("scratch", (PAIRS, ROWS, SQ, KT, ROWS, 2 * QT * SQ), F32, kind="Internal").ap()
    attention_kernel(nc, *args, out, scratch)
    result = run_bass_kernel_spmd(nc, [inputs], core_ids=[0])
    rows = result.results[0]["out"]
    return np.ascontiguousarray(rows.transpose(0, 2, 1, 3)).reshape(B, S, DI)
```

```python
from contextlib import ExitStack

import numpy as np

import concourse.bass as bass
from concourse import mybir

F32 = mybir.dt.float32
F32R = mybir.dt.float32r
I32 = mybir.dt.int32
ALU = mybir.AluOpType
ACT = mybir.ActivationFunctionType

P = 128
B = 8
S = 256
KV = 256
H = 8
D = 256
DI = 256
DL = 192
EPS = 1e-5
SCALE = 1.0 / D ** 0.5

UP = DL - P
PAIRS = H // 2
STEPS = B * PAIRS
QT = S // P
KT = KV // P
IT = DI // P
DT = D // P
PW = 2 * P + 2 * UP
MASKED = -3.0e38
WARMING = 4
LAG = 3
SQ = 32
SQUARES = KV // SQ
ROWS = P // SQ



def attention_kernel(nc, xT, x, ctxT, ctx, mask, wqT, wkT, wvT, wo, gamma, beta, out, scratch):
    es = ExitStack()
    with es:
        def sb(name, shape, dt=F32):
            return es.enter_context(nc.sbuf_tensor(name, shape, dt))

        def bank(name, shape):
            return es.enter_context(nc.psum_tensor(name, shape, F32))

        def sem(name):
            return es.enter_context(nc.semaphore(name))

        wq_raw = sb("wq_raw", [P, H * DT, DI])
        wk_raw = sb("wk_raw", [P, H * DT, DL])
        wv_raw = sb("wv_raw", [P, H * DT, DL])
        wo_raw = sb("wo_raw", [P, H * DT, DI])
        A_hi = sb("A_hi", [P, IT, PAIRS * PW], F32R)
        A_lo = sb("A_lo", [P, IT, PAIRS * PW], F32R)
        CL_hi = sb("CL_hi", [P, H, DI], F32R)
        CL_lo = sb("CL_lo", [P, H, DI], F32R)
        CU_hi = sb("CU_hi", [P, PAIRS, DI], F32R)
        CU_lo = sb("CU_lo", [P, PAIRS, DI], F32R)
        gamma_sb = sb("gamma_sb", [P, DI])
        beta_sb = sb("beta_sb", [P, DI])
        ident = sb("ident", [P, P])
        zeros = sb("zeros", [P, DI])
        eps_col = sb("eps_col", [P, QT])
        power_col = sb("power_col", [P, QT])

        xT_raw = sb("xT_raw", [P, IT, S])
        xT_hi = sb("xT_hi", [P, IT, S], F32R)
        xT_lo = sb("xT_lo", [P, IT, S], F32R)
        ctxT_raw = sb("ctxT_raw", [P, 2, KV])
        ctxT_hi = sb("ctxT_hi", [P, 2, KV], F32R)
        ctxT_lo = sb("ctxT_lo", [P, 2, KV], F32R)
        ctx_raw = sb("ctx_raw", [P, KT, DL])
        ctxL_hi = sb("ctxL_hi", [P, KT, P], F32R)
        ctxL_lo = sb("ctxL_lo", [P, KT, P], F32R)
        ctxU = sb("ctxU", [P, KT, 2 * UP], F32R)
        mask_raw = sb("mask_raw", [P, KV], I32)
        mask_low = sb("mask_low", [P, KV])
        mask_bias = sb("mask_bias", [P, KV])
        x_res = sb("x_res", [P, QT, DI])

        gL_hi = sb("gL_hi", [P, 2, S], F32R)
        gL_lo = sb("gL_lo", [P, 2, S], F32R)
        gU = sb("gU", [P, 2, S], F32R)
        neg_scores = sb("neg_scores", [P, 2 * QT, KV])
        neg_max = sb("neg_max", [P, 2 * QT])
        probs = [sb(f"probs{n}", [P, 2 * QT, KV]) for n in range(2)]
        row_sum = sb("row_sum", [P, 2 * QT])
        inv_sum = sb("inv_sum", [P, 2 * QT])
        squares = sb("squares", [P, SQUARES, 2 * QT, SQ])
        pT_raw = [sb(f"pT_raw{n}", [P, KT, ROWS, 2 * QT, SQ]) for n in range(2)]
        pT_hi = sb("pT_hi", [P, KT, 2, S], F32R)
        pT_lo = sb("pT_lo", [P, KT, 2, S], F32R)
        tL_hi = sb("tL_hi", [P, 2, S], F32R)
        tL_lo = sb("tL_lo", [P, 2, S], F32R)
        tU_moved = sb("tU_moved", [P, S])
        tU = sb("tU", [P, S])
        tU_hi = sb("tU_hi", [P, S], F32R)
        tU_lo = sb("tU_lo", [P, S], F32R)

        y = sb("y", [P, QT, DI])
        y_scaled = sb("y_scaled", [P, QT, DI])
        y_out = sb("y_out", [P, QT, DI])
        stats = sb("stats", [P, QT, 6])
        mean_var = sb("mean_var", [P, QT, 2])
        var_eps = sb("var_eps", [P, QT])
        rstd = sb("rstd", [P, QT])

        score_bank = [bank("score_bank0", [P, QT, KV]), bank("score_bank1", [P, QT, KV])]
        tL_bank = bank("tL_bank", [P, 2, S])
        tU_bank = bank("tU_bank", [P, 2, S])
        gL_bank = bank("gL_bank", [P, 2, S])
        gU_bank = bank("gU_bank", [P, 2, S])
        out_bank = bank("out_bank", [P, QT, DI])
        spare_bank = bank("spare_bank", [P, 2, S])
        fold_banks = [spare_bank, out_bank, tL_bank, tU_bank]
        pT_banks = [gL_bank, gU_bank]

        def places(name, t):
            if not (isinstance(t, int) and t == STEPS - 2):
                return {"pT": (pT_hi[:], pT_lo[:]),
                        "tL": (tL_bank, tL_hi[:], tL_lo[:]),
                        "tU": (tU_bank, tU_hi[:], tU_lo[:])}[name]
            wide = [A[:, 0, 0:KT * 2 * S].rearrange("p (k hh s) -> p k hh s", k=KT, hh=2) for A in (A_hi, A_lo)]
            return {"pT": (wide[0], wide[1]),
                    "tL": (score_bank[0], xT_hi[:], xT_lo[:]),
                    "tU": (score_bank[1], gU[:, 0, :], gU[:, 1, :])}[name]

        def output(t, q):
            if q > 0 and isinstance(t, int) and t >= STEPS - PAIRS:
                return spare_bank[:].rearrange("p a c -> p (a c)")[:, 0:DI]
            return out_bank[:, q, :]

        q_head_in = [sem(f"q_head_in{h}") for h in range(2)]
        q_weights_in = {j: sem(f"q_weights_in{j}") for j in range(1, PAIRS)}
        o_weights_in = [sem(f"o_weights_in{j}") for j in range(PAIRS)]
        affine_in = sem("affine_in")
        xT_in = sem("xT_in")
        ctxT_in = sem("ctxT_in")
        ctx_in = sem("ctx_in")
        mask_in = sem("mask_in")
        x_res_in = sem("x_res_in")
        out_stored = sem("out_stored")
        constants = sem("constants")
        zeros_made = sem("zeros_made")
        A_product = sem("A_product")
        A_hi_done = sem("A_hi_done")
        A_split = sem("A_split")
        C_product = sem("C_product")
        C_hi_done = sem("C_hi_done")
        C_split = sem("C_split")
        xT_hi_done = sem("xT_hi_done")
        xT_split = sem("xT_split")
        ctxT_hi_done = sem("ctxT_hi_done")
        ctxT_split = sem("ctxT_split")
        ctx_hi_done = sem("ctx_hi_done")
        ctx_split = sem("ctx_split")
        mask_lowered = sem("mask_lowered")
        mask_ready = sem("mask_ready")
        g_product = sem("g_product")
        g_hi_done = sem("g_hi_done")
        g_split = sem("g_split")
        scores_done = sem("scores_done")
        max_done = sem("max_done")
        exp_done = sem("exp_done")
        inv_done = sem("inv_done")
        probs_done = sem("probs_done")
        squares_done = sem("squares_done")
        squares_stored = sem("squares_stored")
        pT_in = [sem(f"pT_in{n}") for n in range(2)]
        pT_done = sem("pT_done")
        pT_hi_done = sem("pT_hi_done")
        pT_split = sem("pT_split")
        t_product = sem("t_product")
        t_hi_done = sem("t_hi_done")
        tU_share_moved = sem("tU_share_moved")
        tU_summed = sem("tU_summed")
        t_split = sem("t_split")
        out_product = sem("out_product")
        out_bank_read = sem("out_bank_read")
        stats_done = sem("stats_done")
        mean_done = sem("mean_done")
        var_eps_done = sem("var_eps_done")
        rstd_done = sem("rstd_done")
        y_scaled_done = sem("y_scaled_done")
        y_out_done = sem("y_out_done")
        waits_passed = sem("waits_passed")

        block = es.enter_context(nc.Block())

        def batch_of(src, b):
            if isinstance(b, int):
                return src[b]
            return src[bass.ds(b, 1)].rearrange("o p a c -> p (o a) c")

        @block.sync
        def _(sp):
            def load_xT(b):
                sp.dma_start(xT_raw[:], batch_of(xT, b)).then_inc(xT_in, 16)

            def load_ctxT(b):
                sp.dma_start(ctxT_raw[:], batch_of(ctxT, b)).then_inc(ctxT_in, 16)

            def load_ctx(b):
                sp.dma_start(ctx_raw[:], batch_of(ctx, b)).then_inc(ctx_in, 16)

            def load_x_res(b):
                sp.dma_start(x_res[:], batch_of(x, b)).then_inc(x_res_in, 16)

            def load_mask(b):
                src = mask[b:b + 1] if isinstance(b, int) else mask[bass.ds(b, 1)]
                sp.dma_start(mask_raw[:], src.broadcast_to((P, KV))).then_inc(mask_in, 16)

            def store_out(b):
                sp.wait_ge(y_out_done, QT * b + QT)
                sp.dma_start(batch_of(out, b), y_out[:]).then_inc(out_stored, 16)

            sp.sem_inc(out_stored, 16)
            for j in range(PAIRS):
                if j > 0:
                    tiles = slice(2 * j * DT, 2 * (j + 1) * DT)
                    sp.dma_start(wk_raw[:, tiles], wkT[:, tiles]).then_inc(q_weights_in[j], 16)
                    sp.dma_start(wq_raw[:, tiles], wqT[:, tiles]).then_inc(q_weights_in[j], 16)
                else:
                    for h in range(2):
                        tiles = slice(h * DT, (h + 1) * DT)
                        sp.dma_start(wk_raw[:, tiles], wkT[:, tiles]).then_inc(q_head_in[h], 16)
                    load_xT(0)
            load_ctxT(0)
            load_mask(0)
            load_ctx(0)
            for j in range(PAIRS):
                tiles = slice(2 * j * DT, 2 * (j + 1) * DT)
                sp.dma_start(wv_raw[:, tiles], wvT[:, tiles]).then_inc(o_weights_in[j], 16)
                sp.dma_start(wo_raw[:, tiles], wo[:, tiles]).then_inc(o_weights_in[j], 16)
            load_x_res(0)
            sp.dma_start(gamma_sb[:], gamma.broadcast_to((P, DI))).then_inc(affine_in, 16)
            sp.dma_start(beta_sb[:], beta.broadcast_to((P, DI))).then_inc(affine_in, 16)

            def load_ahead(b):
                sp.wait_ge(xT_split, b)
                load_xT(b)
                sp.wait_ge(ctxT_split, b)
                load_ctxT(b)
                sp.wait_ge(mask_lowered, b)
                load_mask(b)

            def load_ctx_ahead(b):
                sp.wait_ge(ctx_split, 2 * b)
                load_ctx(b)

            def load_residual(b):
                sp.wait_ge(out_bank_read, b + 1)
                load_x_res(b)

            def carry_squares(t, j, raw_free=True):
                sp.wait_ge(squares_done, 2 * QT * t + 2 * QT)
                sp.dma_start(scratch[j].rearrange("i c k jj r -> (i c) (k jj r)"),
                             squares[:].rearrange("p s n r -> p (s n r)")).then_inc(squares_stored, 16)
                sp.wait_ge(squares_stored, 16 * t + 16)
                if raw_free:
                    sp.wait_ge(pT_split, 2 * (t - 2) + 2)
                for jj in range(ROWS):
                    sp.dma_start(pT_raw[j % 2][SQ * jj:SQ * (jj + 1)].rearrange("c k i n r -> c k i (n r)"),
                                 scratch[j][:, :, :, jj, :].rearrange("i c k r -> c k i r")).then_inc(pT_in[j % 2], 16)

            load_ahead(1)
            carry_squares(0, 0, raw_free=False)
            carry_squares(1, 1, raw_free=False)
            carry_squares(2, 2)
            load_ctx_ahead(1)
            carry_squares(3, 3)
            carry_squares(4, 0)
            with sp.Fori(1, B - 1) as b:
                load_ahead(b + 1)
                carry_squares(PAIRS * b + 1, 1)
                carry_squares(PAIRS * b + 2, 2)
                load_ctx_ahead(b + 1)
                carry_squares(PAIRS * b + 3, 3)
                load_residual(b)
                store_out(b - 1)
                carry_squares(PAIRS * b + 4, 0)
            carry_squares(STEPS - 3, 1)
            load_residual(B - 1)
            store_out(B - 2)
            for q in range(QT):
                sp.wait_ge(y_out_done, QT * (B - 1) + 1 + q)
                sp.dma_start(out[B - 1][:, q, :], y_out[:, q, :]).then_inc(out_stored, 16)
            sp.wait_ge(out_stored, 16 * (B + QT))

        @block.tensor
        def _(pe):
            def split_products(into, pairs, first=True, last=True, shared=False):
                for n, (stationary, moving) in enumerate(pairs):
                    ins = nc.tensor.matmul(into, stationary, moving, start=first and n == 0,
                                           stop=last and n == len(pairs) - 1, skip_group_check=shared)
                return ins

            def fold_A(h):
                if h < 2:
                    pe.wait_ge(q_head_in[h], 32)
                elif h % 2 == 0:
                    pe.wait_ge(q_weights_in[h // 2], 32)
                if h >= len(fold_banks):
                    pe.wait_ge(A_split, 2 * (h - len(fold_banks)) + 2)
                dst = fold_banks[h % len(fold_banks)][:].rearrange("p a c -> p (a c)")
                for i in range(IT):
                    for d in range(DT):
                        ins = nc.tensor.matmul(dst[:, i * DL:(i + 1) * DL],
                                               wq_raw[:, h * DT + d, i * P:(i + 1) * P],
                                               wk_raw[:, h * DT + d, :], start=d == 0, stop=d == DT - 1)
                ins.then_inc(A_product, 1)

            def fold_C(j):
                pe.wait_ge(o_weights_in[j], 32)
                if j == 0:
                    pe.wait_ge(A_split, 2 * H)
                if j >= 2:
                    pe.wait_ge(C_split, 2 * (j - 2) + 2)
                lower, upper = fold_banks[2 * (j % 2)], fold_banks[2 * (j % 2) + 1]
                for hh in range(2):
                    h = 2 * j + hh
                    for d in range(DT):
                        ins = nc.tensor.matmul(lower[:, hh, :], wv_raw[:, h * DT + d, 0:P],
                                               wo_raw[:, h * DT + d, :], start=d == 0, stop=d == DT - 1)
                ins.then_inc(C_product, 1)
                for hh in range(2):
                    h = 2 * j + hh
                    for d in range(DT):
                        ins = nc.tensor.matmul(upper[hh * UP:(hh + 1) * UP, 0, :],
                                               wv_raw[:, h * DT + d, P:DL],
                                               wo_raw[:, h * DT + d, :], start=d == 0, stop=d == DT - 1)
                ins.then_inc(C_product, 1)

            def query_products(t, j, b):
                if j == 0:
                    pe.wait_ge(xT_split, b + 1)
                col = j * PW

                def tile(into, at):
                    pairs = []
                    for i in range(IT):
                        hi, lo = A_hi[:, i, at:at + P], A_lo[:, i, at:at + P]
                        pairs += [(hi, xT_hi[:, i, :]), (hi, xT_lo[:, i, :]), (lo, xT_hi[:, i, :])]
                    return split_products(into, pairs)

                tile(gU_bank[:, 0, :], col + 2 * P).then_inc(g_product, 1)
                tile(gL_bank[:, 0, :], col)
                tile(gL_bank[:, 1, :], col + P).then_inc(g_product, 1)

            def scores(t, j, b, heads=(0, 1)):
                if j == 0:
                    pe.wait_ge(ctxT_split, b + 1)
                for hh in heads:
                    if hh == 0:
                        pe.wait_ge(g_hi_done, 3 * t + 3)
                        pe.wait_ge(g_split, 3 * t + 2)
                    for q in range(QT):
                        rows = slice(q * P, (q + 1) * P)
                        hi, lo, up = gL_hi[:, hh, rows], gL_lo[:, hh, rows], gU[:, hh, rows]
                        split_products(score_bank[hh][:, q, :],
                                       [(up, ctxT_hi[:, 1, :]), (up, ctxT_lo[:, 1, :]),
                                        (hi, ctxT_hi[:, 0, :]), (hi, ctxT_lo[:, 0, :])], last=False)
                        if hh == 0 and q == 0:
                            pe.wait_ge(g_split, 3 * t + 3)
                        ins = split_products(score_bank[hh][:, q, :], [(lo, ctxT_hi[:, 0, :])], first=False)
                    ins.then_inc(scores_done, 1)

            def transposes(t):
                for hh in range(2):
                    pe.wait_ge(probs_done, 2 * t + 1 + hh)
                    if t == STEPS - 1:
                        pe.wait_ge(pT_split, 2 * t - 1 + hh)
                    for k in range(KT):
                        for q in range(QT):
                            ins = nc.tensor.transpose(pT_banks[hh][:, k, q * P:(q + 1) * P],
                                                      probs[t % 2][:, hh * QT + q, k * P:(k + 1) * P],
                                                      ident[:])
                    ins.then_inc(pT_done, 1)

            def context_products(t, j, b):
                if j == 0:
                    pe.wait_ge(C_split, 2 * PAIRS)
                    pe.wait_ge(ctx_split, 2 * b + 2)
                (hi, lo), tL, tU = places("pT", t), places("tL", t)[0], places("tU", t)[0]
                pe.wait_ge(pT_hi_done, 2 * t + 2)
                split_products(tL[:], [(part[:, k, :], hi[:, k]) for k in range(KT) for part in (ctxL_hi, ctxL_lo)],
                               last=False)
                split_products(tU[:], [(ctxU[:, k, :], hi[:, k]) for k in range(KT)], last=False)
                by_squares = not (isinstance(t, int) and t >= STEPS - 2)
                for k in range(KT):
                    pe.wait_ge(pT_split, 2 * t + (k + 1 if by_squares else 2))
                    end = k == KT - 1
                    lower = split_products(tL[:], [(ctxL_hi[:, k, :], lo[:, k])], first=False, last=end)
                    if end:
                        lower.then_inc(t_product, 1)
                    upper = split_products(tU[:], [(ctxU[:, k, :], lo[:, k])], first=False, last=end)
                upper.then_inc(t_product, 1)

            def output_products(t, j, b):
                (_, L_hi, L_lo), (_, U_hi, U_lo) = places("tL", t), places("tU", t)

                def lower(q):
                    rows = slice(q * P, (q + 1) * P)
                    pairs = []
                    for hh in range(2):
                        hi, lo, h = L_hi[:, hh, rows], L_lo[:, hh, rows], 2 * j + hh
                        pairs += [(hi, CL_hi[:, h]), (hi, CL_lo[:, h]), (lo, CL_hi[:, h])]
                    own = isinstance(t, int) and t >= STEPS - PAIRS
                    split_products(output(t, q), pairs, first=j == 0 and (q == 0 or own), last=False, shared=True)

                def upper(q):
                    rows = slice(q * P, (q + 1) * P)
                    hi, lo = U_hi[:, rows], U_lo[:, rows]
                    pairs = [(hi, CU_hi[:, j]), (hi, CU_lo[:, j]), (lo, CU_hi[:, j])]
                    return split_products(output(t, q), pairs, first=False, last=j == PAIRS - 1, shared=True)

                if j == 0:
                    pe.wait_ge(out_bank_read, b + 1)
                pe.wait_ge(t_split, 2 * t + 1)
                lower(0)
                if isinstance(t, int) and t == STEPS - 1:
                    pe.wait_ge(t_split, 2 * t + 2)
                    upper(0).then_inc(out_product, 1)
                    lower(1)
                    upper(1).then_inc(out_product, 1)
                    return
                lower(1)
                pe.wait_ge(t_split, 2 * t + 2)
                upper(0)
                upper(1).then_inc(out_product, 1)

            def step(t, j, b, folds=()):
                before = not (isinstance(t, int) and t < LAG)
                jb, bb = (j - LAG) % PAIRS, b - 1 if j < LAG else b
                ja, ba = (j + 1) % PAIRS, b + 1 if j == PAIRS - 1 else b
                scores(t, j, b)
                if before:
                    context_products(t - LAG, jb, bb)
                query_products(t + 1, ja, ba)
                if before:
                    output_products(t - LAG, jb, bb)
                for pair in folds:
                    fold_C(pair)

            pe.wait_ge(zeros_made, 1)
            for _ in range(WARMING):
                nc.tensor.matmul(score_bank[0][:, 0, :], zeros[:, 0:P], zeros[:], start=True, stop=True)
            for h in range(H - 2):
                fold_A(h)
            pe.wait_ge(A_split, 4)
            query_products(0, 0, 0)
            for h in range(H - 2, H):
                fold_A(h)
            step(0, 0, 0, folds=[0])
            step(1, 1, 0, folds=[1])
            step(2, 2, 0, folds=[2, 3])
            for t in range(LAG, PAIRS + 2):
                step(t, t % PAIRS, t // PAIRS)
            with pe.Fori(1, B - 1) as b:
                step(PAIRS * b + 2, 2, b)
                step(PAIRS * b + 3, 3, b)
                step(PAIRS * b + 4, 0, b + 1)
                step(PAIRS * b + 5, 1, b + 1)
            step(STEPS - 2, 2, B - 1)
            scores(STEPS - 1, 3, B - 1, heads=[0])
            context_products(STEPS - 4, 0, B - 1)
            scores(STEPS - 1, 3, B - 1, heads=[1])
            pe.wait_ge(constants, 3)
            transposes(STEPS - 2)
            output_products(STEPS - 4, 0, B - 1)
            context_products(STEPS - 3, 1, B - 1)
            transposes(STEPS - 1)
            context_products(STEPS - 2, 2, B - 1)
            output_products(STEPS - 3, 1, B - 1)
            context_products(STEPS - 1, 3, B - 1)
            output_products(STEPS - 2, 2, B - 1)
            output_products(STEPS - 1, 3, B - 1)

        @block.scalar
        def _(act):
            def hi_part(dst, src):
                return nc.scalar.activation(dst, src, ACT.Copy)

            def A_hi_part(h):
                act.wait_ge(A_product, h + 1)
                src = fold_banks[h % len(fold_banks)][:].rearrange("p a c -> p (a c)")[:, 0:IT * DL] \
                    .rearrange("p (i f) -> p i f", i=IT)
                low = (h // 2) * PW + (h % 2) * P
                up = (h // 2) * PW + 2 * P + (h % 2) * UP
                hi_part(A_hi[:, :, low:low + P], src[:, :, 0:P]).then_inc(A_hi_done, 1)
                hi_part(A_hi[:, :, up:up + UP], src[:, :, P:DL]).then_inc(A_hi_done, 1)

            def C_hi_part(j):
                lower, upper = fold_banks[2 * (j % 2)], fold_banks[2 * (j % 2) + 1]
                act.wait_ge(C_product, 2 * j + 1)
                hi_part(CL_hi[:, 2 * j:2 * j + 2, :], lower[:]).then_inc(C_hi_done, 1)
                act.wait_ge(C_product, 2 * j + 2)
                hi_part(CU_hi[:, j, :], upper[:, 0, :]).then_inc(C_hi_done, 1)

            def ctxT_hi_part(b):
                act.wait_ge(ctxT_in, 16 * b + 16)
                hi_part(ctxT_hi[:], ctxT_raw[:]).then_inc(ctxT_hi_done, 1)

            def gU_hi_part(t):
                act.wait_ge(g_product, 2 * t + 1)
                hi_part(gU[0:UP, 0, :], gU_bank[0:UP, 0, :]).then_inc(g_hi_done, 1)
                hi_part(gU[UP:P, 1, :], gU_bank[UP:P, 0, :]).then_inc(g_hi_done, 1)

            def gL_hi_part(t):
                act.wait_ge(g_product, 2 * t + 2)
                hi_part(gL_hi[:], gL_bank[:]).then_inc(g_hi_done, 1)

            def exponentials(t, j, heads=(0, 1)):
                if not (isinstance(t, int) and t < 2):
                    act.wait_ge(squares_done, 2 * QT * (t - 1))
                for n in [QT * hh + q for hh in heads for q in range(QT)]:
                    act.wait_ge(max_done, 4 * t + 1 + n)
                    nc.scalar.activation(probs[j % 2][:, n, :], neg_scores[:, n, :], ACT.Exp,
                                         bias=neg_max[:, n:n + 1], scale=-1.0,
                                         accum_out=row_sum[:, n:n + 1]).then_inc(exp_done, 1)

            def xT_hi_part(b):
                act.wait_ge(xT_in, 16 * b + 16)
                hi_part(xT_hi[:], xT_raw[:]).then_inc(xT_hi_done, 1)

            def pT_hi_part(t, j):
                if isinstance(t, int) and t >= STEPS - 2:
                    for hh in range(2):
                        act.wait_ge(pT_done, 2 * (t - STEPS + 2) + 1 + hh)
                        hi_part(places("pT", t)[0][:, :, hh, :], pT_banks[hh][:]).then_inc(pT_hi_done, 1)
                    return
                act.wait_ge(pT_in[j % 2], 16 * ROWS // 2 * (t - j % 2) + 16 * ROWS)
                for k in range(KT):
                    hi_part(pT_hi[:, k].rearrange("p hh (q i r) -> p (hh q) i r", q=QT, i=ROWS),
                            pT_raw[j % 2][:, k].rearrange("p i n r -> p n i r")).then_inc(pT_hi_done, 1)

            def ctx_hi_part(b):
                act.wait_ge(ctx_in, 16 * b + 16)
                lower, upper = ctx_raw[:, :, 0:P], ctx_raw[:, :, P:DL]
                hi_part(ctxL_hi[:], lower).then_inc(ctx_hi_done, 1)
                hi_part(ctxU[:, :, 0:UP], upper).then_inc(ctx_hi_done, 1)

            def t_hi_part(t):
                act.wait_ge(t_product, 2 * t + 1)
                L_bank, L_hi, _ = places("tL", t)
                hi_part(L_hi, L_bank[:]).then_inc(t_hi_done, 1)
                act.wait_ge(t_product, 2 * t + 2)
                U_bank = places("tU", t)[0]
                nc.scalar.activation(tU_moved[0:UP, :], U_bank[UP:P, 0, :], ACT.Copy).then_inc(tU_share_moved, 1)
                nc.scalar.activation(tU_moved[UP:P, :], U_bank[0:UP, 1, :], ACT.Copy).then_inc(tU_share_moved, 1)

            def tU_hi_part(t):
                act.wait_ge(tU_summed, 2 * t + 2)
                hi_part(places("tU", t)[1], tU[:]).then_inc(t_hi_done, 1)

            def step(t, j, b, folds=()):
                before = not (isinstance(t, int) and t < LAG)
                exponentials(t, j)
                if before:
                    t_hi_part(t - LAG)
                if j == PAIRS - 1:
                    ctxT_hi_part(b + 1)
                gU_hi_part(t + 1)
                if before:
                    tU_hi_part(t - LAG)
                gL_hi_part(t + 1)
                if j == 2:
                    if not (isinstance(b, int) and b == B - 1):
                        xT_hi_part(b + 1)
                    ctx_hi_part(b)
                for pair in folds:
                    C_hi_part(pair)
                if not (isinstance(t, int) and t < LAG - 1):
                    pT_hi_part(t - LAG + 1, (j - LAG + 1) % PAIRS)

            for h in range(2):
                tiles = slice(h * DT, (h + 1) * DT)
                act.dma_start(wq_raw[:, tiles], wqT[:, tiles]).then_inc(q_head_in[h], 16)
            A_hi_part(0)
            A_hi_part(1)
            xT_hi_part(0)
            for h in range(2, H - 2):
                A_hi_part(h)
            gU_hi_part(0)
            gL_hi_part(0)
            ctxT_hi_part(0)
            for h in range(H - 2, H):
                A_hi_part(h)
            step(0, 0, 0, folds=[0])
            step(1, 1, 0, folds=[1])
            step(2, 2, 0, folds=[2, 3])
            for t in range(LAG, PAIRS + 2):
                step(t, t % PAIRS, t // PAIRS)
            with act.Fori(1, B - 1) as b:
                step(PAIRS * b + 2, 2, b)
                step(PAIRS * b + 3, 3, b)
                step(PAIRS * b + 4, 0, b + 1)
                step(PAIRS * b + 5, 1, b + 1)
            step(STEPS - 2, 2, B - 1)
            exponentials(STEPS - 1, 3, heads=[0])
            t_hi_part(STEPS - 4)
            tU_hi_part(STEPS - 4)
            pT_hi_part(STEPS - 3, 1)
            exponentials(STEPS - 1, 3, heads=[1])
            pT_hi_part(STEPS - 2, 2)
            t_hi_part(STEPS - 3)
            tU_hi_part(STEPS - 3)
            pT_hi_part(STEPS - 1, 3)
            for t in (STEPS - 2, STEPS - 1):
                t_hi_part(t)
                tU_hi_part(t)

        @block.vector
        def _(dve):
            def waited():
                dve.sem_inc(waits_passed, 1)

            def lo_part(dst, whole, hi):
                return nc.vector.tensor_tensor(dst, whole, hi.bitcast(F32), ALU.subtract)

            def A_lo_part(h):
                src = fold_banks[h % len(fold_banks)][:].rearrange("p a c -> p (a c)")[:, 0:IT * DL] \
                    .rearrange("p (i f) -> p i f", i=IT)
                low = (h // 2) * PW + (h % 2) * P
                up = (h // 2) * PW + 2 * P + (h % 2) * UP
                dve.wait_ge(A_hi_done, 2 * h + 2)
                lo_part(A_lo[:, :, low:low + P], src[:, :, 0:P], A_hi[:, :, low:low + P]).then_inc(A_split, 1)
                lo_part(A_lo[:, :, up:up + UP], src[:, :, P:DL], A_hi[:, :, up:up + UP]).then_inc(A_split, 1)

            def C_lo_part(j):
                lower, upper = fold_banks[2 * (j % 2)], fold_banks[2 * (j % 2) + 1]
                dve.wait_ge(C_hi_done, 2 * j + 1)
                lo_part(CL_lo[:, 2 * j:2 * j + 2, :], lower[:], CL_hi[:, 2 * j:2 * j + 2, :]).then_inc(C_split, 1)
                dve.wait_ge(C_hi_done, 2 * j + 2)
                lo_part(CU_lo[:, j, :], upper[:, 0, :], CU_hi[:, j, :]).then_inc(C_split, 1)

            def lower_mask(b):
                dve.wait_ge(mask_in, 16 * b + 16)
                nc.vector.tensor_scalar(mask_low[:], mask_raw[:], 0, MASKED, ALU.is_equal,
                                        ALU.mult).then_inc(mask_lowered, 1)

            def finish_mask(b):
                dve.wait_ge(mask_lowered, b + 1)
                nc.vector.tensor_scalar(mask_bias[:], mask_low[:], 4.0, None, ALU.mult).then_inc(mask_ready, 1)

            def ctx_lo_part(b):
                dve.wait_ge(ctx_hi_done, 2 * b + 2)
                lower, upper = ctx_raw[:, :, 0:P], ctx_raw[:, :, P:DL]
                lo_part(ctxL_lo[:], lower, ctxL_hi[:]).then_inc(ctx_split, 1)
                lo_part(ctxU[:, :, UP:2 * UP], upper, ctxU[:, :, 0:UP]).then_inc(ctx_split, 1)

            def gU_lo_part(t, hh):
                dve.wait_ge(g_hi_done, 3 * t + 1 + hh)
                own, other = (slice(0, UP), slice(UP, P))[::1 if hh == 0 else -1]
                lo_part(gU[other, hh, :], gU_bank[own, 0, :], gU[own, hh, :]).then_inc(g_split, 1)

            def gL_lo_part(t):
                dve.wait_ge(g_hi_done, 3 * t + 3)
                lo_part(gL_lo[:], gL_bank[:], gL_hi[:]).then_inc(g_split, 1)

            def maxima(t, b, heads=(0, 1)):
                for hh in heads:
                    dve.wait_ge(mask_ready, b + 1)
                    dve.wait_ge(scores_done, 2 * t + 1 + hh)
                    waited()
                    for q in range(QT):
                        n = hh * QT + q
                        nc.vector.tensor_tensor_reduce(
                            out=neg_scores[:, n, :], in0=score_bank[hh][:, q, :], in1=mask_bias[:],
                            scale=-SCALE, scalar=3.0e38, op0=ALU.add, op1=ALU.min,
                            accum_out=neg_max[:, n:n + 1]).then_inc(max_done, 1)

            def inverse_sum(t, hh):
                if isinstance(t, int) and t == STEPS - 1:
                    dve.wait_ge(probs_done, 2 * t - 1 + hh)
                dve.wait_ge(exp_done, 4 * t + QT * (hh + 1))
                nc.vector.reciprocal(inv_sum[:, QT * hh:QT * hh + QT],
                                     row_sum[:, QT * hh:QT * hh + QT]).then_inc(inv_done, 1)

            def transpose_squares(t, j):
                if not (isinstance(t, int) and t == 0):
                    dve.wait_ge(squares_stored, 16 * t)
                dve.wait_ge(probs_done, 2 * t + 2)
                for n in range(2 * QT):
                    nc.vector.transpose(squares[:, :, n, :],
                                        probs[j % 2][:, n, :].rearrange("p (s c) -> p s c", c=SQ)) \
                        .then_inc(squares_done, 1)

            def pT_lo_part(t):
                if t == STEPS - 2:
                    dve.wait_ge(pT_split, 2 * t)
                for hh in range(2):
                    dve.wait_ge(pT_hi_done, 2 * t + 1 + hh)
                    hi, lo = places("pT", t)
                    lo_part(lo[:, :, hh, :], pT_banks[hh][:], hi[:, :, hh, :]).then_inc(pT_split, 1)

            def t_lo_part_lower(t):
                dve.wait_ge(t_hi_done, 2 * t + 1)
                L_bank, L_hi, L_lo = places("tL", t)
                lo_part(L_lo, L_bank[:], L_hi).then_inc(t_split, 1)

            def tU_sum(t):
                if isinstance(t, int) and t >= STEPS - 2:
                    dve.wait_ge(t_split, 2 * t)
                dve.wait_ge(tU_share_moved, 2 * t + 2)
                for hh, part in enumerate((slice(0, UP), slice(UP, P))):
                    nc.vector.tensor_tensor(tU[part, :], places("tU", t)[0][part, hh, :], tU_moved[part, :],
                                            ALU.add).then_inc(tU_summed, 1)

            def t_lo_part_upper(t):
                dve.wait_ge(t_hi_done, 2 * t + 2)
                _, U_hi, U_lo = places("tU", t)
                lo_part(U_lo, tU[:], U_hi).then_inc(t_split, 1)

            def add_residual(b):
                dve.wait_ge(x_res_in, 16 * b + 16)
                dve.wait_ge(out_product, PAIRS * b + PAIRS)
                nc.vector.tensor_tensor(y[:], out_bank[:], x_res[:], ALU.add).then_inc(out_bank_read, 1)

            def statistics(b):
                dve.wait_ge(out_bank_read, b + 2)
                for q in range(QT):
                    nc.vector.bn_stats(stats[:, q, :], y[:, q, :]).then_inc(stats_done, 1)
                for q in range(QT):
                    dve.wait_ge(stats_done, QT * b + q + 1)
                    waited()
                    nc.vector.bn_aggr(mean_var[:, q, :], stats[:, q, :]).then_inc(mean_done, 1)

            def centre_tile(q):
                nc.vector.scalar_tensor_tensor(
                    y_scaled[:, q, :], y[:, q, :], mean_var[:, q, 0:1], gamma_sb[:],
                    ALU.subtract, ALU.mult).then_inc(y_scaled_done, 1)

            def normalise_tile(b, q):
                dve.wait_ge(y_scaled_done, QT * b + q + 1)
                nc.vector.scalar_tensor_tensor(
                    y_out[:, q, :], y_scaled[:, q, :], rstd[:, q:q + 1], beta_sb[:],
                    ALU.mult, ALU.add).then_inc(y_out_done, 1)

            def centre(b):
                for q in range(QT):
                    if q == 0:
                        dve.wait_ge(mean_done, QT * b + QT)
                    centre_tile(q)

            def normalise(b):
                dve.wait_ge(rstd_done, b + 1)
                dve.wait_ge(out_stored, 16 * b + 16)
                for q in range(QT):
                    normalise_tile(b, q)

            def step(t, j, b, ends=None, folds=()):
                before = not (isinstance(t, int) and t < LAG)
                by_squares = not (isinstance(t, int) and t >= STEPS - 2)
                maxima(t, b)
                if ends is not None and j == 3:
                    add_residual(ends)
                inverse_sum(t, 0)
                if ends is not None and j == 3:
                    statistics(ends)
                if ends is not None and j == 0:
                    centre(ends)
                inverse_sum(t, 1)
                if ends is not None and j == 0:
                    normalise(ends)
                if j == 2 and not (isinstance(b, int) and b == B - 1):
                    lower_mask(b + 1)
                if j == 3:
                    finish_mask(b + 1)
                if before:
                    t_lo_part_lower(t - LAG)
                    tU_sum(t - LAG)
                gU_lo_part(t + 1, 0)
                if before:
                    t_lo_part_upper(t - LAG)
                gU_lo_part(t + 1, 1)
                gL_lo_part(t + 1)
                if by_squares:
                    transpose_squares(t, j)
                if j == 2:
                    ctx_lo_part(b)
                for pair in folds:
                    C_lo_part(pair)

            dve.sem_inc(out_bank_read, 1)
            for h in range(H - 2):
                A_lo_part(h)
            gU_lo_part(0, 0)
            gU_lo_part(0, 1)
            gL_lo_part(0)
            for h in range(H - 2, H):
                A_lo_part(h)
            lower_mask(0)
            finish_mask(0)
            step(0, 0, 0, folds=[0])
            step(1, 1, 0, folds=[1])
            step(2, 2, 0, folds=[2, 3])
            dve.wait_ge(affine_in, 32)
            for t in range(LAG, PAIRS + 2):
                step(t, t % PAIRS, t // PAIRS)
            with dve.Fori(1, B - 1) as b:
                step(PAIRS * b + 2, 2, b)
                step(PAIRS * b + 3, 3, b, ends=b - 1)
                step(PAIRS * b + 4, 0, b + 1, ends=b - 1)
                step(PAIRS * b + 5, 1, b + 1)
            step(STEPS - 2, 2, B - 1)

            def t_lo_parts(t):
                t_lo_part_lower(t)
                tU_sum(t)
                t_lo_part_upper(t)

            add_residual(B - 2)
            maxima(STEPS - 1, B - 1, heads=[0])
            inverse_sum(STEPS - 1, 0)
            t_lo_parts(STEPS - 4)
            maxima(STEPS - 1, B - 1, heads=[1])
            statistics(B - 2)
            inverse_sum(STEPS - 1, 1)
            pT_lo_part(STEPS - 2)
            t_lo_parts(STEPS - 3)
            pT_lo_part(STEPS - 1)
            centre(B - 2)
            normalise(B - 2)
            t_lo_parts(STEPS - 2)
            t_lo_parts(STEPS - 1)
            for q in range(QT):
                dve.wait_ge(out_product, STEPS + q)
                if q == 0:
                    dve.wait_ge(x_res_in, 16 * B)
                nc.vector.tensor_tensor(y[:, q, :], output(STEPS - 1, q), x_res[:, q, :], ALU.add) \
                    .then_inc(out_bank_read, 1)
                dve.wait_ge(out_bank_read, B + 1 + q)
                nc.vector.bn_stats(stats[:, q, :], y[:, q, :]).then_inc(stats_done, 1)
                dve.wait_ge(stats_done, QT * (B - 1) + 1 + q)
                nc.vector.bn_aggr(mean_var[:, q, :], stats[:, q, :]).then_inc(mean_done, 1)
                dve.wait_ge(mean_done, QT * (B - 1) + 1 + q)
                centre_tile(q)
            dve.wait_ge(out_stored, 16 * B)
            for q in range(QT):
                dve.wait_ge(rstd_done, B + q)
                normalise_tile(B - 1, q)

        @block.gpsimd
        def _(pool):
            nc.gpsimd.memset(zeros[:], 0.0).then_inc(zeros_made, 1)
            nc.gpsimd.memset(ident[:], 0.0).then_inc(constants, 1)
            nc.gpsimd.memset(eps_col[:], EPS)
            nc.gpsimd.memset(power_col[:], -0.5).then_inc(constants, 1)
            pool.wait_ge(constants, 2)
            nc.gpsimd.affine_select(out=ident[:], in_=ident[:], compare_op=ALU.not_equal, fill=1.0, base=0,
                                    pattern=[[-1, P]], channel_multiplier=1).then_inc(constants, 1)

            def normalise_probs(t, j, heads=(0, 1)):
                for hh in heads:
                    rows = slice(QT * hh, QT * hh + QT)
                    inv = inv_sum[:, rows].rearrange("p (n o) -> p n o", o=1).broadcast_to((P, QT, KV))
                    pool.wait_ge(inv_done, 2 * t + 1 + hh)
                    nc.gpsimd.tensor_tensor(probs[j % 2][:, rows, :], probs[j % 2][:, rows, :], inv, ALU.mult) \
                        .then_inc(probs_done, 1)

            def deviation(b):
                pool.wait_ge(mean_done, QT * b + QT)
                nc.gpsimd.tensor_tensor(var_eps[:], mean_var[:, :, 1], eps_col[:], ALU.add).then_inc(var_eps_done, 1)
                pool.wait_ge(var_eps_done, b + 1)
                nc.gpsimd.tensor_tensor(rstd[:], var_eps[:], power_col[:], ALU.pow).then_inc(rstd_done, 1)

            def lo_part(dst, whole, hi):
                return nc.gpsimd.tensor_tensor(dst, whole, hi.bitcast(F32), ALU.subtract)

            def xT_lo_part(b):
                pool.wait_ge(xT_hi_done, b + 1)
                lo_part(xT_lo[:], xT_raw[:], xT_hi[:]).then_inc(xT_split, 1)

            def pT_lo_part(t, j):
                for k in range(KT):
                    pool.wait_ge(pT_hi_done, 2 * t + 1 + k)
                    nc.gpsimd.tensor_tensor(
                        pT_lo[:, k].rearrange("p hh (q i r) -> p (hh q) i r", q=QT, i=ROWS),
                        pT_raw[j % 2][:, k].rearrange("p i n r -> p n i r"),
                        pT_hi[:, k].rearrange("p hh (q i r) -> p (hh q) i r", q=QT, i=ROWS).bitcast(F32),
                        ALU.subtract).then_inc(pT_split, 1)

            def ctxT_lo_part(b):
                pool.wait_ge(ctxT_hi_done, b + 1)
                lo_part(ctxT_lo[:], ctxT_raw[:], ctxT_hi[:]).then_inc(ctxT_split, 1)

            def step(t, j, b, ends=None):
                normalise_probs(t, j)
                if j == PAIRS - 1 and not (isinstance(b, int) and b == B - 1):
                    ctxT_lo_part(b + 1)
                if ends is not None:
                    deviation(ends)
                if j == 2 and not (isinstance(b, int) and b == B - 1):
                    xT_lo_part(b + 1)
                if not (isinstance(t, int) and t < LAG - 1):
                    pT_lo_part(t - LAG + 1, (j - LAG + 1) % PAIRS)

            xT_lo_part(0)
            ctxT_lo_part(0)
            for t in range(PAIRS + 2):
                step(t, t % PAIRS, t // PAIRS)
            with pool.Fori(1, B - 1) as b:
                step(PAIRS * b + 2, 2, b)
                step(PAIRS * b + 3, 3, b, ends=b - 1)
                step(PAIRS * b + 4, 0, b + 1)
                step(PAIRS * b + 5, 1, b + 1)
            step(STEPS - 2, 2, B - 1)
            normalise_probs(STEPS - 1, 3, heads=[0])
            pT_lo_part(STEPS - 3, 1)
            normalise_probs(STEPS - 1, 3, heads=[1])
            deviation(B - 2)
            for q in range(QT):
                col = slice(q, q + 1)
                pool.wait_ge(mean_done, QT * (B - 1) + 1 + q)
                nc.gpsimd.tensor_tensor(var_eps[:, col], mean_var[:, q, 1:2], eps_col[:, col], ALU.add) \
                    .then_inc(var_eps_done, 1)
                pool.wait_ge(var_eps_done, B + q)
                nc.gpsimd.tensor_tensor(rstd[:, col], var_eps[:, col], power_col[:, col], ALU.pow) \
                    .then_inc(rstd_done, 1)


def kernel(x, ctx_768, mask_BxS2_if1, L0_xattn_Wq, L0_xattn_Wk, L0_xattn_Wv, L0_xattn_Wo, L0_xattn_gamma,
           L0_xattn_beta):
    import concourse.bacc as bacc
    from concourse.bass_utils import run_bass_kernel_spmd

    def tiles(a):
        *lead, rows, cols = a.shape
        return np.ascontiguousarray(np.moveaxis(a.reshape(*lead, rows // P, P, cols), -3, -2))

    x, ctx, mask = np.asarray(x), np.asarray(ctx_768), np.asarray(mask_BxS2_if1)
    wq, wk, wv, wo = (np.asarray(w) for w in (L0_xattn_Wq, L0_xattn_Wk, L0_xattn_Wv, L0_xattn_Wo))
    ctxT = ctx.transpose(0, 2, 1)
    arrays = {
        "xT": tiles(x.transpose(0, 2, 1)),
        "x": tiles(x),
        "ctxT": tiles(np.concatenate([ctxT, ctxT[:, P:]], axis=1)),
        "ctx": tiles(ctx),
        "mask": np.ascontiguousarray(mask),
        "wqT": tiles(wq.T),
        "wkT": tiles(wk.T),
        "wvT": tiles(wv.T),
        "wo": tiles(wo),
        "gamma": np.asarray(L0_xattn_gamma).reshape(1, DI),
        "beta": np.asarray(L0_xattn_beta).reshape(1, DI),
    }
    nc = bacc.Bacc("TRN2", target_bir_lowering=False, num_devices=1)
    inputs = {f"in_{name}": a for name, a in arrays.items()}
    args = [nc.dram_tensor(name, a.shape, mybir.dt.from_np(a.dtype), kind="ExternalInput").ap()
            for name, a in inputs.items()]
    out = nc.dram_tensor("out", (B, P, QT, DI), F32, kind="ExternalOutput").ap()
    scratch = nc.dram_tensor("scratch", (PAIRS, ROWS, SQ, KT, ROWS, 2 * QT * SQ), F32, kind="Internal").ap()
    attention_kernel(nc, *args, out, scratch)
    result = run_bass_kernel_spmd(nc, [inputs], core_ids=[0])
    rows = result.results[0]["out"]
    return np.ascontiguousarray(rows.transpose(0, 2, 1, 3)).reshape(B, S, DI)
```
